# Optimizing a Trainium2 kernel written in Bass

```python
import numpy as np
import jax
import jax.numpy as jnp

def _softmax(x, axis=-1):
    return jax.nn.softmax(x, axis=axis)

def _gelu(x):
    return jax.nn.gelu(x, approximate=True)

def _silu(x):
    return jax.nn.silu(x)

def _sigmoid(x):
    return jax.nn.sigmoid(x)

def _layernorm(x, axis=-1, eps=1e-05):
    m = jnp.mean(x, axis=axis, keepdims=True)
    v = jnp.var(x, axis=axis, keepdims=True)
    return (x - m) / jnp.sqrt(v + eps)

def _scatter_add(tgt, idx, src, axis=0):
    return tgt.at[idx].add(src)

def _segment_sum(src, seg, n):
    return jax.ops.segment_sum(src, seg, n)
kernel_name = 'mk_adj_preln_d4_adj_r2_6b5d63'

def setup_inputs(seed: int=0):
    np.random.seed(seed)
    _w = jnp.asarray

    def _rec_inputs():
        import jax
        import jax.numpy as jnp
        _gk = jax.random.key(seed)
        x = -0.000929 + 1 * jax.random.normal(jax.random.fold_in(_gk, 1), (8, 2048, 64), jnp.float32)
        _w = (1.0 + jnp.arange(2048, dtype=jnp.float32)) ** (-0.5)
        _w = _w / _w.mean()
        _pij = jnp.clip(0.000976562 * _w[:, None] * _w[None, :], 0.0, 1.0)
        _a = jax.random.uniform(jax.random.fold_in(_gk, 2), (8, 2048, 2048)) < _pij
        _a = jnp.logical_or(_a, jnp.eye(2048, dtype=bool))
        _af = _a.astype(jnp.float32)
        _af = _af * jax.random.uniform(jax.random.fold_in(_gk, 3), (8, 2048, 2048), jnp.float32, 0.05, 1)
        adj = _af
        return (x, adj)
    x, adj = _rec_inputs()

    def _L0_gnn_setup():
        import jax, jax.numpy as jnp
        import numpy as np
        B, N, C, R = (4, 2048, 64, 16)
        EPS = 1e-12
        key = jax.random.key(seed)
        k_x, k_w, k_u = jax.random.split(key, 3)
        x = jax.random.normal(k_x, (B, N, C), dtype=jnp.float32)
        W = jax.random.uniform(k_w, (B, N, N), dtype=jnp.float32)
        U = 0.01 * jax.random.normal(k_u, (N, R), dtype=jnp.float32)
        w_scale = jnp.asarray(1.0, dtype=jnp.float32)
        return {'x': x, 'W': W, 'U': U, 'w_scale': w_scale}
    _L0_gnn_all = _L0_gnn_setup()
    _L0_gnn_in = {k: v for k, v in _L0_gnn_all.items() if k in ('U', 'w_scale')}
    del _L0_gnn_all

    def _L1_gnn_setup():
        import jax, jax.numpy as jnp
        import numpy as np
        key = jax.random.key(seed)
        k1, k2 = jax.random.split(key)
        B, N, D = (16, 1024, 64)
        nodes = jax.random.normal(k1, (B, N, D), dtype=jnp.float32)
        edges = jax.random.uniform(k2, (B, N, N), dtype=jnp.float32)
        return {'nodes': nodes, 'edges': edges}
    _L1_gnn_all = _L1_gnn_setup()
    _L1_gnn_in = {k: v for k, v in _L1_gnn_all.items() if k in ()}
    del _L1_gnn_all

    def _L2_gnn_setup():
        import jax, jax.numpy as jnp
        import numpy as np
        B, N, C = (8, 1024, 64)
        N_LAYERS = 3

        def _graph_conv(X, A, Wm, Ws, b):
            M = jnp.einsum('bnc,oc->bno', X, Wm)
            M = jnp.matmul(A, M)
            return M + jnp.einsum('bnc,oc->bno', X, Ws) + b
        key = jax.random.key(seed)
        ks = jax.random.split(key, 2 + 3 * N_LAYERS)
        X = jax.random.normal(ks[0], (B, N, C), dtype=jnp.float32)
        A = jax.random.uniform(ks[1], (B, N, N), dtype=jnp.float32)
        inp = {'X': X, 'A': A}
        bound_w = np.sqrt(3.0) * (np.sqrt(2.0 / (1.0 + 5.0)) / np.sqrt(C))
        bound_b = 1.0 / np.sqrt(C)
        for l in range(N_LAYERS):
            inp[f'Wm{l}'] = jax.random.uniform(ks[2 + 3 * l], (C, C), minval=-bound_w, maxval=bound_w, dtype=jnp.float32)
            inp[f'Ws{l}'] = jax.random.uniform(ks[3 + 3 * l], (C, C), minval=-bound_w, maxval=bound_w, dtype=jnp.float32)
            inp[f'b{l}'] = jax.random.uniform(ks[4 + 3 * l], (C,), minval=-bound_b, maxval=bound_b, dtype=jnp.float32)
        return inp
    _L2_gnn_all = _L2_gnn_setup()
    _L2_gnn_in = {k: v for k, v in _L2_gnn_all.items() if k in ('Wm0', 'Ws0', 'b0', 'Wm1', 'Ws1', 'b1', 'Wm2', 'Ws2', 'b2')}
    del _L2_gnn_all

    def _L3_gnn_setup():
        import jax, jax.numpy as jnp
        import numpy as np
        key = jax.random.key(seed)
        k1, k2 = jax.random.split(key)
        B, N, D = (8, 2048, 64)
        x = jax.random.normal(k1, (B, N, D), dtype=jnp.float32)
        A = jax.random.uniform(k2, (B, N, N), dtype=jnp.float32)
        return {'x': x, 'A': A}
    _L3_gnn_all = _L3_gnn_setup()
    _L3_gnn_in = {k: v for k, v in _L3_gnn_all.items() if k in ()}
    del _L3_gnn_all
    return {'x': x, 'adj': adj, 'L0_gnn_U': _L0_gnn_in['U'], 'L0_gnn_w_scale': _L0_gnn_in['w_scale'], 'L2_gnn_Wm0': _L2_gnn_in['Wm0'], 'L2_gnn_Ws0': _L2_gnn_in['Ws0'], 'L2_gnn_b0': _L2_gnn_in['b0'], 'L2_gnn_Wm1': _L2_gnn_in['Wm1'], 'L2_gnn_Ws1': _L2_gnn_in['Ws1'], 'L2_gnn_b1': _L2_gnn_in['b1'], 'L2_gnn_Wm2': _L2_gnn_in['Wm2'], 'L2_gnn_Ws2': _L2_gnn_in['Ws2'], 'L2_gnn_b2': _L2_gnn_in['b2']}

def reference(x, adj, L0_gnn_U, L0_gnn_w_scale, L2_gnn_Wm0, L2_gnn_Ws0, L2_gnn_b0, L2_gnn_Wm1, L2_gnn_Ws1, L2_gnn_b1, L2_gnn_Wm2, L2_gnn_Ws2, L2_gnn_b2):
    import jax
    import jax.numpy as jnp

    def _L0_gnn_ref(x, W, U, w_scale):
        import jax, jax.numpy as jnp
        import numpy as np
        B, N, C, R = (4, 2048, 64, 16)
        EPS = 1e-12
        Ws = 0.5 * (W + jnp.swapaxes(W, -1, -2))
        A = jax.nn.sigmoid(U @ U.T)
        K = Ws * A[None, :, :]
        deg = jnp.maximum(K.sum(axis=-1), EPS)
        d = jax.lax.rsqrt(deg)
        K = K * d[:, :, None] * d[:, None, :]
        return w_scale * jnp.einsum('bnm,bmc->bnc', K, x)

    def _L1_gnn_ref(nodes, edges):
        import jax, jax.numpy as jnp
        import numpy as np
        N = nodes.shape[1]
        A = edges + jnp.eye(N, dtype=edges.dtype)
        num = jnp.einsum('bij,bjd->bid', A, nodes)
        denom = jnp.sum(A, axis=2, keepdims=True)
        out = num / denom
        return jnp.where(jnp.isnan(out), jnp.zeros_like(out), out)

    def _L2_gnn_ref(X, A, Wm0, Ws0, b0, Wm1, Ws1, b1, Wm2, Ws2, b2):
        import jax, jax.numpy as jnp
        import numpy as np
        B, N, C = (8, 1024, 64)
        N_LAYERS = 3

        def _graph_conv(X, A, Wm, Ws, b):
            M = jnp.einsum('bnc,oc->bno', X, Wm)
            M = jnp.matmul(A, M)
            return M + jnp.einsum('bnc,oc->bno', X, Ws) + b
        H = jax.nn.relu(_graph_conv(X, A, Wm0, Ws0, b0))
        H = jax.nn.relu(_graph_conv(H, A, Wm1, Ws1, b1))
        H = _graph_conv(H, A, Wm2, Ws2, b2)
        return H

    def _L3_gnn_ref(x, A):
        import jax, jax.numpy as jnp
        import numpy as np
        deg = jnp.clip(jnp.sum(A, axis=2, keepdims=True), 1.0, None)
        A_norm = A / deg
        messages = jnp.matmul(A_norm, x)
        return messages
    h = jnp.maximum(_layernorm(x, axis=-1), 0.0)
    x = x + _L0_gnn_ref(h, adj, L0_gnn_U, L0_gnn_w_scale)
    h = jnp.maximum(_layernorm(x, axis=-1), 0.0)
    x = x + _L1_gnn_ref(h, adj)
    h = jnp.maximum(_layernorm(x, axis=-1), 0.0)
    x = x + _L2_gnn_ref(h, adj, L2_gnn_Wm0, L2_gnn_Ws0, L2_gnn_b0, L2_gnn_Wm1, L2_gnn_Ws1, L2_gnn_b1, L2_gnn_Wm2, L2_gnn_Ws2, L2_gnn_b2)
    h = jnp.maximum(_layernorm(x, axis=-1), 0.0)
    x = x + _L3_gnn_ref(h, adj)
    return x

_drawn_inputs = setup_inputs


def setup_inputs(seed=0):
    import zlib

    import numpy as np

    out = dict(_drawn_inputs(seed))
    spreads = {}
    factors = {'L0_gnn_U': 64.0}
    for name, (base, spread) in spreads.items():
        noise = np.random.default_rng([zlib.crc32(name.encode()), seed]).standard_normal(out[name].shape)
        drawn = base * np.exp(spread * noise) if base else spread * noise
        out[name] = jnp.asarray(drawn.astype(out[name].dtype))
    for name, factor in factors.items():
        out[name] = (out[name] * factor).astype(out[name].dtype)
    return out
```

```python
import concourse.bass as bass
from concourse import mybir
from contextlib import ExitStack

F32 = mybir.dt.float32
F16 = mybir.dt.float16
ALU = mybir.AluOpType
ACT = mybir.ActivationFunctionType
AX = mybir.AxisListType

P = 128
CHUNK = 512
LN_EPS = 1e-05
DEG_EPS = 1e-12

A_SCALE = 2.0 ** 8
LO = 2.0 ** 11
DVE_STEPS = 298
T_DEG, T_NORM, T_CONV = 8, 0, 4

GROUPS = [(0, 0), (0, 1), (0, 2), (1, 0), (1, 1), (1, 2), (0, 3), (1, 3),
          (2, 0), (2, 1), (2, 2), (2, 3), (3, 0), (3, 1), (3, 2), (3, 3)]

CONV_IN, CONV_MID, CONV_OUT, ROWS = "conv_in", "conv_mid", "conv_out", "rows"
PRODUCTS = [CONV_IN, CONV_MID, CONV_MID, CONV_OUT, ROWS]
AT = {
    CONV_IN: [(7, 8, 11, 12), (8, 9, 13, 14), (12, 13, 16, 17), (16, 17, 20, 21)],
    CONV_MID: [(7, 8), (8, 9), (12, 13), (16, 17)],
    CONV_OUT: [(7, 8), (8, 9), (12, 13), (16, 17)],
    ROWS: [(7, 8), (8, 9), (12, 13), (16, 17)],
}
NORMED = (-1, 0, 3)


def graph_stack(nc, x, adj, U, w_scale, wm, ws, bias, out):
    B, N, C = x.shape
    R = U.shape[1]
    T = N // P
    J = N // CHUNK
    TJ = T // J
    H = N // 2
    L = len(wm)
    UNITS = T * 2
    CH = T * J

    s_dram = nc.dram_tensor("similarity", (N, N), F32, kind="Internal").ap()
    x_v = x.rearrange("b (t p) c -> b p t c", p=P)
    out_v = out.rearrange("b (t p) c -> b p t c", p=P)

    ctx = ExitStack()
    with ctx:
        def sb(name, shape, dt=F32):
            return ctx.enter_context(nc.sbuf_tensor(name, shape, dt))

        def pb(name):
            return ctx.enter_context(nc.psum_tensor(name, [P, CHUNK], F32))

        def sem(name):
            return ctx.enter_context(nc.semaphore(name))

        ahi = sb("ahi", [P, T, N], F16)
        alo = sb("alo", [P, T, N], F16)
        wrow = sb("wrow", [P, 2, H])
        wcol = sb("wcol", [P, 2, T // 2, P])
        srow = sb("srow", [P, 2, H])
        tsum = sb("tsum", [P, 3, CHUNK])
        kfull = sb("kfull", [P, 3, CHUNK])
        khi = sb("khi", [P, 2, N], F16)
        klo = sb("klo", [P, 2, N], F16)
        stat = sb("stat", [P, 2, T, 2 * C], F16)
        statk = sb("statk", [P, 2, 2 * C], F16)
        xn = sb("xn", [P, T, C])
        hs = sb("hs", [P, T, C])
        hT = sb("hT", [C, N])
        fold_lo = sb("fold_lo", [C, CHUNK])
        fold = sb("fold", [C, 2, CHUNK])
        tmp = sb("tmp", [P, TJ, C])
        tmp2 = sb("tmp2", [P, TJ, C])
        xs = sb("xs", [P, C])
        ident = sb("ident", [P, P])
        ones = sb("ones", [1, P])
        small = sb("small", [P, 8, TJ])
        tiny = sb("tiny", [P, 8])
        rbig = sb("rbig", [P, 2, T])
        kdeg = sb("kdeg", [P, T, J])
        rsum = sb("rsum", [P, T, 2])
        coef0 = sb("coef0", [P, T])
        coef1 = sb("coef1", [P, T])
        coef3 = sb("coef3", [P, T])
        wraw = sb("wraw", [C, 2 * L, C])
        wmT = sb("wmT", [C, L, C])
        wsT = sb("wsT", [C, L, C])
        bcol = sb("bcol", [C, L])
        uraw = sb("uraw", [P, T, R])
        uT = hT[0:R, :]
        w1 = sb("w1", [1, 1])
        wtwo = sb("wtwo", [P, 1])

        kacc = [pb(f"kacc{j}") for j in range(J)]
        pacc = [pb(f"pacc{j}") for j in range(2)]
        tbank = pb("tbank")
        misc = pb("misc")

        def alpha(p):
            return 2.0 ** (T_DEG if p < 0 else T_CONV if 1 <= p <= L else T_NORM) / A_SCALE

        def mslot(g):
            return (misc, tbank)[g % 2][:, 0:TJ * C]

        def mrows(g):
            return mslot(g).rearrange("p (t c) -> p t c", c=C)

        wload = sem("weights_loaded")
        xload = sem("x_loaded")
        wrow_in = [sem(f"row_half_loaded{i}") for i in range(2)]
        wcol_in = [sem(f"strip_half_loaded{i}") for i in range(2)]
        srow_in = [sem(f"similarity_half_loaded{i}") for i in range(2)]
        out_done = sem("out_stored")
        sim_stored = [sem(f"similarity_slot_stored{i}") for i in range(8)]
        const_ready = sem("constants_ready")
        pro_pe = sem("prologue_pe")
        pro_dve = sem("prologue_dve")
        sim_logits = sem("similarity_logits")
        sim_sig = sem("similarity_sigmoid")
        sim_ready = sem("similarity_scaled")
        turned = sem("strip_turned")
        ahi_ready = sem("ahi_ready")
        alo_ready = sem("alo_ready")
        summed = sem("rows_summed")
        tsum_ready = sem("tsum_ready")
        k_ready = sem("k_ready")
        khi_ready = sem("khi_ready")
        klo_ready = sem("klo_ready")
        deg_ready = sem("deg_ready")
        deg_root = sem("deg_root")
        statk_ready = sem("statk_ready")
        k_used = sem("k_used")
        prod_done = sem("product_chunk_done")
        lo_ready = sem("fold_lo_ready")
        fold_ready = sem("fold_ready")
        bias_added = sem("bias_added")
        ln_var = sem("variance_ready")
        ln_root = sem("variance_root")
        hs_ready = sem("hs_ready")
        xhi_ready = sem("xhi_ready")
        stat_ready = sem("stat_ready")
        hT_ready = sem("hT_ready")
        misc_full = sem("misc_full")
        misc_free = sem("misc_freed_by_vector")
        x_final = sem("x_final")
        pe_passed = sem("tensor_engine_passed")
        dve_step = sem("dve_step")

        MISC = J + 3 * J + J + J + J + J
        HS = 4 * J
        FOLDS = 6 * J
        tring = [tbank, pacc[0], pacc[1]]

        block = ctx.enter_context(nc.Block())

        after = [[[] for _ in GROUPS] for _ in range(len(PRODUCTS) + 1)]
        for p, kind in enumerate(PRODUCTS):
            for c, at in enumerate(AT[kind]):
                names = {CONV_IN: ("fold", "rows", "hT", "msg"), CONV_MID: ("fold", "msg")}
                for name, g in zip(names.get(kind, ("fold", "rows")), at):
                    after[p + g // 16][g % 16].append((name, p, c))
        first = [(name, -1, c) for c in range(J) for name in ("fold", "rows")]
        steps = first + [s for p in after for g in p for s in g]

        def number(kinds):
            return {s: n for n, s in enumerate(s for s in steps if s[0] in kinds)}

        use = number(("rows", "hT", "msg"))
        assert len(use) == MISC and MISC % 2 == 0
        row_no = number(("rows",))
        fold_no = number(("fold",))
        hT_no = {s: n for n, s in enumerate(
            s for s in steps if s[0] == "hT" or (s[0] == "fold" and s[1] >= 0
                                                           and PRODUCTS[s[1]] == CONV_MID))}
        norm_no = {s: n for n, s in enumerate(s for s in steps if s[0] == "rows" and s[1] in NORMED)}
        stat_steps = [s for s in steps if s[0] == "msg" or (s[0] == "rows" and s[1] in (-1, 3))]
        stat_no = {s: n for n, s in enumerate(stat_steps)}
        stat_of = {((s[1] + 1), s[2]): n for s, n in stat_no.items()}
        ROWS_N, HT_N, STAT_N = len(row_no), len(hT_no), len(stat_no)
        used_by = {n: s for s, n in use.items()}

        @block.sync
        def _(sp):
            for i in range(L):
                sp.dma_start(wraw[:, 2 * i, :], wm[i]).then_inc(wload, 16)
                sp.dma_start(wraw[:, 2 * i + 1, :], ws[i]).then_inc(wload, 16)
                sp.dma_start(bcol[:, i:i + 1], bias[i]).then_inc(wload, 16)
            sp.dma_start(uraw[:, :, :], U.rearrange("(t p) r -> p t r", p=P)).then_inc(wload, 16)
            sp.dma_start(w1[:, :], w_scale).then_inc(wload, 16)
            sp.sem_inc(out_done, 1)
            for u in range(UNITS):
                sp.wait_ge(sim_ready, u + 1)
                i, h = u // 2, u % 2
                sp.dma_start(s_dram[i * P:(i + 1) * P, h * H:(h + 1) * H],
                             alo[:, T // 2 + u % 8, :].bitcast(F32)).then_inc(sim_stored[u % 8], 16)
            for done in sim_stored:
                sp.wait_ge(done, 16 * UNITS // 8)

            with sp.Fori(0, B) as b:
                sp.wait_ge(out_done, 1 + b * (16 * J))
                sp.dma_start(xn[:, :, :], x_v[b]).then_inc(xload, 16)
                for u in range(UNITS):
                    i, h = u // 2, u % 2
                    done = 1 + b * CH + max(0, 2 * (u - 1))
                    sp.wait_ge(turned, done)
                    sp.dma_start(wcol[:, u % 2, :, :],
                                 adj[b, h * H:(h + 1) * H, i * P:(i + 1) * P]
                                 .rearrange("(t p) m -> p t m", p=P)).then_inc(wcol_in[u % 2], 16)
                    sp.wait_ge(tsum_ready, done)
                    sp.dma_start(wrow[:, u % 2, :], adj[b, i * P:(i + 1) * P, h * H:(h + 1) * H])\
                        .then_inc(wrow_in[u % 2], 16)
                    sp.wait_ge(k_ready, done)
                    sp.dma_start(srow[:, u % 2, :], s_dram[i * P:(i + 1) * P, h * H:(h + 1) * H])\
                        .then_inc(srow_in[u % 2], 16)
                for c in range(J):
                    sp.wait_ge(x_final, b * J + c + 1)
                    sp.dma_start(out_v[b, :, c * TJ:(c + 1) * TJ, :], xn[:, c * TJ:(c + 1) * TJ, :])\
                        .then_inc(out_done, 16)
            sp.wait_ge(out_done, 1 + B * 16 * J)

        @block.gpsimd
        def _(pool):
            nc.gpsimd.memset(ident[:, :], 0.0).then_inc(const_ready, 1)
            nc.gpsimd.memset(ones[:, :], 1.0).then_inc(const_ready, 1)
            pool.wait_ge(const_ready, 2)
            nc.gpsimd.affine_select(out=ident[:, :], in_=ident[:, :], compare_op=ALU.not_equal, fill=1.0,
                                    base=0, pattern=[[-1, P]], channel_multiplier=1).then_inc(const_ready, 1)
            pool.sem_inc(k_ready, 1)
            with pool.Fori(0, B) as b:
                for q in range(CH):
                    u = q // 2
                    if q % 2 == 0:
                        pool.wait_ge(srow_in[u % 2], b * (16 * T) + 16 * (u // 2 + 1))
                    pool.wait_ge(tsum_ready, 1 + b * CH + q + 1)
                    pool.wait_ge(klo_ready, 1 + b * CH + max(0, q - 2))
                    o = (q % 2) * CHUNK
                    nc.gpsimd.tensor_tensor(kfull[:, q % 3, :], tsum[:, q % 3, :],
                                            srow[:, u % 2, o:o + CHUNK], ALU.mult).then_inc(k_ready, 1)

        @block.scalar
        def _(act):
            for q in range(CH):
                act.wait_ge(sim_logits, q + 1)
                u = q // 2
                if u >= 8:
                    act.wait_ge(sim_stored[u % 8], 16 * (u // 8))
                o = (q % 2) * CHUNK
                nc.scalar.activation(alo[:, T // 2 + u % 8, :].bitcast(F32)[:, o:o + CHUNK],
                                     kacc[q % J][:, :], ACT.Sigmoid).then_inc(sim_sig, 1)

            with act.Fori(0, B) as b:
                fold_n = [0]

                def root_ln(n):
                    act.wait_ge(ln_var, b * HS + n + 1)
                    nc.scalar.activation(small[:, 2, :], small[:, 1, :], ACT.Sqrt).then_inc(ln_root, 1)

                def khigh(q):
                    act.wait_ge(k_ready, 1 + b * CH + q + 1)
                    i, j = q // J, q % J
                    if j == 0:
                        act.wait_ge(k_used, 1 + b * T + max(0, i - 1))
                    nc.scalar.activation(khi[:, i % 2, j * CHUNK:(j + 1) * CHUNK], kfull[:, q % 3, :],
                                         ACT.Copy, accum_out=kdeg[:, i, j:j + 1]).then_inc(khi_ready, 1)

                def deg_sqrt(i):
                    act.wait_ge(deg_ready, b * T + i + 1)
                    nc.scalar.activation(tiny[:, 2:3], tiny[:, 1:2], ACT.Sqrt).then_inc(deg_root, 1)

                def xhigh(src_ap, p, c):
                    nc.scalar.activation(stat[:, p % 2, c * TJ:(c + 1) * TJ, 0:C], src_ap, ACT.Copy,
                                         scale=1.0 / LO).then_inc(xhi_ready, 1)

                def hs_high(n, p, c):
                    act.wait_ge(hs_ready, b * HS + n + 1)
                    xhigh(hs[:, c * TJ:(c + 1) * TJ, :], p, c)

                for c in range(J):
                    root_ln(c)
                for q in range(CH):
                    i, j, u = q // J, q % J, q // 2
                    if q % 2 == 0:
                        act.wait_ge(wrow_in[u % 2], b * (16 * T) + 16 * (u // 2 + 1))
                        nc.scalar.activation(wrow[:, u % 2, :], wrow[:, u % 2, :], ACT.Copy,
                                             accum_out=rsum[:, i, u % 2:u % 2 + 1]).then_inc(summed, 1)
                    act.wait_ge(turned, 1 + b * CH + q + 1)
                    nc.scalar.activation(ahi[:, i, j * CHUNK:(j + 1) * CHUNK], tring[q % 3][:, :], ACT.Copy,
                                         scale=A_SCALE).then_inc(ahi_ready, 1)
                    if q >= 1:
                        khigh(q - 1)
                    if j == 3 and i >= 1:
                        deg_sqrt(i - 1)
                khigh(CH - 1)
                deg_sqrt(T - 1)

                for step in steps:
                    name, p, c = step
                    if name == "fold":
                        n = fold_no[step]
                        if p < 0:
                            act.wait_ge(k_used, 1 + b * T + T)
                        else:
                            act.wait_ge(prod_done, 1 + b * (FOLDS - J) + p * J + c + 1)
                        act.wait_ge(fold_ready, 1 + b * FOLDS + n)
                        src = kacc[c] if p < 0 else pacc[c % 2]
                        nc.scalar.activation(fold_lo[:, :], src[C:2 * C, :], ACT.Copy,
                                             scale=alpha(p) / LO).then_inc(lo_ready, 1)
                        if step in hT_no:
                            act.wait_ge(fold_ready, 1 + b * FOLDS + n + 1)
                            nc.scalar.activation(hT[:, c * CHUNK:(c + 1) * CHUNK], fold[:, n % 2, :], ACT.Relu,
                                                 bias=bcol[:, p - 1:p]).then_inc(hT_ready, 1)
                        if p == L:
                            act.wait_ge(fold_ready, 1 + b * FOLDS + n + 1)
                            nc.scalar.activation(fold[:, n % 2, :], fold[:, n % 2, :], ACT.Identity,
                                                 bias=bcol[:, L - 1:L]).then_inc(bias_added, 1)
                    if name == "rows" and step in norm_no:
                        root_ln(J + norm_no[step])
                        if step in stat_no:
                            hs_high(J + norm_no[step], p + 1, c)
                    if name == "hT":
                        m = use[step]
                        act.wait_ge(misc_full, b * MISC + m + 1)
                        to = hT[:, c * CHUNK:(c + 1) * CHUNK].rearrange("c (k e n) -> c k e n", e=2, n=P)
                        for e in range(2):
                            mm = nc.scalar.activation(
                                to[:, :, e, :], mslot(m)[e * C:(e + 1) * C, :]
                                .rearrange("c (k n) -> c k n", n=P), ACT.Copy, scale=1.0 / LO)
                        mm.then_inc(hT_ready, 1)
                    if name == "msg":
                        act.wait_ge(misc_full, b * MISC + use[step] + 1)
                        xhigh(mrows(use[step]), p + 1, c)

        @block.vector
        def _(dve):
            dve.wait_ge(pro_pe, 1)
            for i in range(L):
                nc.vector.tensor_scalar(wmT[:, i, :], pacc[0][0:C, 2 * i * C:(2 * i + 1) * C],
                                        LO / 2.0 ** T_CONV, None, ALU.mult)
                nc.vector.tensor_scalar(wsT[:, i, :], pacc[0][0:C, (2 * i + 1) * C:(2 * i + 2) * C],
                                        A_SCALE / 2.0 ** T_CONV, None, ALU.mult)
            nc.vector.tensor_scalar(wtwo[:, :], pacc[1][:, 0:1], 2.0, None, ALU.mult).then_inc(pro_dve, 1)
            for j in range(J):
                dve.wait_ge(pro_pe, 2 + j)
                nc.vector.tensor_copy(uT[:, j * CHUNK:(j + 1) * CHUNK], kacc[j][0:R, :]).then_inc(pro_dve, 1)
            dve.wait_ge(pro_dve, 1 + J)
            for u in range(UNITS):
                dve.wait_ge(sim_sig, 2 * u + 2)
                v = alo[:, T // 2 + u % 8, :].bitcast(F32)
                nc.vector.tensor_scalar(v, v, A_SCALE / 2, None, ALU.mult).then_inc(sim_ready, 1)
            for done in sim_stored:
                dve.wait_ge(done, 16 * UNITS // 8)

            for s in (tsum_ready, alo_ready, klo_ready, fold_ready, misc_free):
                dve.sem_inc(s, 1)
            with dve.Fori(0, B) as b:
                count = [0]

                def then(ins):
                    count[0] += 1
                    ins.then_inc(dve_step, 1)
                    dve.wait_ge(dve_step, b * DVE_STEPS + count[0])

                def half_rstd(v, s, r, t):
                    then(nc.vector.reciprocal(r, s))
                    then(nc.vector.tensor_tensor(t, v, r, ALU.mult))
                    then(nc.vector.tensor_tensor(t, t, s, ALU.add))
                    then(nc.vector.reciprocal(r, t))

                def wide(v):
                    return v.unsqueeze(2).to_broadcast([P, TJ, C])

                def norm(n, c):
                    xc, hc = xn[:, c * TJ:(c + 1) * TJ, :], hs[:, c * TJ:(c + 1) * TJ, :]
                    s0, s1, s2, s3, s4 = (small[:, k, :] for k in range(5))
                    then(nc.vector.tensor_reduce(s0, xc, AX.X, ALU.add))
                    then(nc.vector.tensor_scalar(s3, s0, -1.0 / C, None, ALU.mult))
                    then(nc.vector.tensor_tensor(hc, xc, wide(s3), ALU.add))
                    then(nc.vector.tensor_tensor(tmp[:, :, :], hc, hc, ALU.mult))
                    then(nc.vector.tensor_reduce(s0, tmp[:, :, :], AX.X, ALU.add))
                    nc.vector.tensor_scalar(s1, s0, 1.0 / C, LN_EPS, ALU.mult, ALU.add).then_inc(ln_var, 1)
                    dve.wait_ge(ln_root, b * HS + n + 1)
                    half_rstd(s1, s2, s3, s4)
                    then(nc.vector.tensor_tensor(hc, hc, wide(s3), ALU.mult))
                    nc.vector.tensor_scalar(hc, hc, 0.0, 2.0 * LO, ALU.max, ALU.mult).then_inc(hs_ready, 1)
                    dve.wait_ge(hs_ready, b * HS + n + 1)

                dve.wait_ge(xload, b * 16 + 16)
                for c in range(J):
                    norm(c, c)

                def klow(q):
                    i, j = q // J, q % J
                    dve.wait_ge(khi_ready, b * CH + q + 1)
                    o = j * CHUNK
                    nc.vector.tensor_tensor(klo[:, i % 2, o:o + CHUNK], kfull[:, q % 3, :],
                                            khi[:, i % 2, o:o + CHUNK], ALU.subtract).then_inc(klo_ready, 1)

                def degree(i):
                    then(nc.vector.tensor_reduce(tiny[:, 0:1], kdeg[:, i, :], AX.X, ALU.add))
                    nc.vector.tensor_scalar(tiny[:, 1:2], tiny[:, 0:1], 1.0 / A_SCALE, DEG_EPS,
                                            ALU.mult, ALU.max).then_inc(deg_ready, 1)

                def scaled_rows(i):
                    dve.wait_ge(deg_root, b * T + i + 1)
                    half_rstd(tiny[:, 1:2], tiny[:, 2:3], coef0[:, i:i + 1], tiny[:, 3:4])
                    then(nc.vector.tensor_scalar(xs[:, :], hs[:, i, :], coef0[:, i:i + 1],
                                                 2.0 / 2.0 ** T_DEG, ALU.mult, ALU.mult))
                    dve.wait_ge(k_used, 1 + b * T + max(0, i - 1))
                    then(nc.vector.tensor_scalar(statk[:, i % 2, 0:C], xs[:, :], 1.0 / LO, None, ALU.mult))
                    nc.vector.scalar_tensor_tensor(statk[:, i % 2, C:2 * C], statk[:, i % 2, 0:C], -LO,
                                                   xs[:, :], ALU.mult, ALU.add).then_inc(statk_ready, 1)

                for q in range(CH):
                    i, j, u = q // J, q % J, q // 2
                    o = (q % 2) * CHUNK
                    dve.wait_ge(summed, b * UNITS + u + 1)
                    dve.wait_ge(ahi_ready, b * CH + q + 1)
                    dve.wait_ge(k_ready, 1 + b * CH + max(0, q - 2))
                    nc.vector.tensor_tensor(tsum[:, q % 3, :], tring[q % 3][:, :],
                                            wrow[:, u % 2, o:o + CHUNK], ALU.add).then_inc(tsum_ready, 1)
                    nc.vector.scalar_tensor_tensor(alo[:, i, j * CHUNK:(j + 1) * CHUNK], tring[q % 3][:, :],
                                                   A_SCALE, ahi[:, i, j * CHUNK:(j + 1) * CHUNK],
                                                   ALU.mult, ALU.subtract).then_inc(alo_ready, 1)
                    if q >= 2:
                        klow(q - 2)
                    if j == 1 and i >= 1:
                        degree(i - 1)
                    if j == 2 and i >= 1:
                        scaled_rows(i - 1)
                klow(CH - 2)
                klow(CH - 1)
                degree(T - 1)
                scaled_rows(T - 1)

                dve.wait_ge(statk_ready, b * T + T)
                then(nc.vector.tensor_scalar(coef0[:, :], coef0[:, :], wtwo[:, 0:1], None, ALU.mult))
                then(nc.vector.tensor_reduce(rbig[:, 0, :], rsum[:, :, :], AX.X, ALU.add))
                then(nc.vector.tensor_scalar(coef1[:, :], rbig[:, 0, :], 1.0, None, ALU.add))
                then(nc.vector.reciprocal(coef1[:, :], coef1[:, :]))
                then(nc.vector.tensor_scalar(coef3[:, :], rbig[:, 0, :], 1.0, None, ALU.max))
                then(nc.vector.reciprocal(coef3[:, :], coef3[:, :]))

                def release(step, ins):
                    ins.then_inc(misc_free, 1)
                    dve.wait_ge(misc_free, 1 + b * ROWS_N + row_no[step] + 1)

                for step in steps:
                    name, p, c = step
                    sl = slice(c * TJ, (c + 1) * TJ)
                    if name == "fold":
                        n = fold_no[step]
                        dve.wait_ge(lo_ready, b * FOLDS + n + 1)
                        if n >= 2:
                            before = next(s for s in steps if s in fold_no and fold_no[s] == n - 2)
                            if before in hT_no:
                                dve.wait_ge(hT_ready, b * HT_N + hT_no[before] + 1)
                            else:
                                dve.wait_ge(misc_full, b * MISC + use[("rows",) + before[1:]] + 1)
                        src = kacc[c] if p < 0 else pacc[c % 2]
                        nc.vector.scalar_tensor_tensor(fold[:, n % 2, :], src[0:C, :], alpha(p), fold_lo[:, :],
                                                       ALU.mult, ALU.add).then_inc(fold_ready, 1)
                    if name == "rows":
                        y, xc, t, t2 = mrows(use[step]), xn[:, sl, :], tmp[:, :, :], tmp2[:, :, :]
                        dve.wait_ge(misc_full, b * MISC + use[step] + 1)
                        if p == -1:
                            release(step, nc.vector.tensor_tensor(t, y, wide(coef0[:, sl]), ALU.mult))
                        elif p == 0:
                            release(step, nc.vector.scalar_tensor_tensor(t, hs[:, sl, :], 1.0 / LO, y,
                                                                         ALU.mult, ALU.add))
                            then(nc.vector.tensor_tensor(t, t, wide(coef1[:, sl]), ALU.mult))
                            then(nc.vector.tensor_scalar(t2, t, 0.0, None, ALU.min))
                            then(nc.vector.scalar_tensor_tensor(t, t, 0.0, t2, ALU.max, ALU.add))
                        elif p == 4:
                            release(step, nc.vector.tensor_tensor(t, y, wide(coef3[:, sl]), ALU.mult))
                        if p == 3:
                            release(step, nc.vector.tensor_tensor(xc, xc, y, ALU.add))
                        elif p == 4:
                            nc.vector.tensor_tensor(xc, xc, t, ALU.add).then_inc(x_final, 1)
                        else:
                            then(nc.vector.tensor_tensor(xc, xc, t, ALU.add))
                        if step in norm_no:
                            norm(J + norm_no[step], c)
                    if step in stat_no:
                        dve.wait_ge(xhi_ready, b * STAT_N + stat_no[step] + 1)
                        st = stat[:, (p + 1) % 2, sl, :]
                        src = mrows(use[step]) if name == "msg" else hs[:, sl, :]
                        nc.vector.scalar_tensor_tensor(st[:, :, C:2 * C], st[:, :, 0:C], -LO, src,
                                                       ALU.mult, ALU.add).then_inc(stat_ready, 1)
                assert count[0] == DVE_STEPS, count[0]

        @block.tensor
        def _(pe):
            pe.wait_ge(wload, 16 * (3 * L + 2))
            pe.wait_ge(const_ready, 3)
            for k in range(2 * L):
                nc.tensor.transpose(pacc[0][0:C, k * C:(k + 1) * C], wraw[:, k, :], ident[0:C, 0:C])
            nc.tensor.matmul(pacc[1][:, 0:1], ones[:, :], w1[:, :], start=True, stop=True).then_inc(pro_pe, 1)
            for j in range(J):
                for k in range(TJ):
                    mm = nc.tensor.transpose(kacc[j][0:R, k * P:(k + 1) * P], uraw[:, j * TJ + k, :], ident[:, :])
                mm.then_inc(pro_pe, 1)
            pe.wait_ge(pro_dve, 1 + J)
            for q in range(CH):
                if q >= J:
                    pe.wait_ge(sim_sig, q - J + 1)
                i, j = q // J, q % J
                nc.tensor.matmul(kacc[j][:, :], uT[:, i * P:(i + 1) * P], uT[:, j * CHUNK:(j + 1) * CHUNK],
                                 start=True, stop=True).then_inc(sim_logits, 1)
            pe.wait_ge(sim_sig, CH)

            for s in (turned, k_used, prod_done):
                pe.sem_inc(s, 1)
            with pe.Fori(0, B) as b:
                def k_product(i):
                    pe.wait_ge(statk_ready, b * T + i + 1)
                    pe.wait_ge(klo_ready, 1 + b * CH + (i + 1) * J)
                    for part, k in ((khi, 0), (klo, 1)):
                        for j in range(J):
                            mm = nc.tensor.matmul(kacc[j][:, :], statk[:, i % 2, :],
                                                  part[:, i % 2, j * CHUNK:(j + 1) * CHUNK],
                                                  start=(i == 0 and k == 0), stop=(i == T - 1 and k == 1))
                    mm.then_inc(k_used, 1)

                pe.wait_ge(fold_ready, 1 + b * FOLDS)
                pe.wait_ge(misc_free, 1 + b * ROWS_N)
                for q in range(CH):
                    u = q // 2
                    if q % 2 == 0:
                        pe.wait_ge(wcol_in[u % 2], b * (16 * T) + 16 * (u // 2 + 1))
                    pe.wait_ge(alo_ready, 1 + b * CH + max(0, q - 2))
                    for k in range(TJ):
                        mm = nc.tensor.transpose(tring[q % 3][:, k * P:(k + 1) * P],
                                                 wcol[:, u % 2, (q % 2) * TJ + k, :], ident[:, :])
                    mm.then_inc(turned, 1)
                    if q % J == 2 and q // J >= 2:
                        k_product(q // J - 2)
                k_product(T - 2)
                k_product(T - 1)

                def slot_ready(m):
                    if m < 2:
                        return
                    s = used_by[m - 2]
                    if s[0] == "rows":
                        pe.wait_ge(misc_free, 1 + b * ROWS_N + row_no[s] + 1)
                    elif s[0] == "msg":
                        pe.wait_ge(stat_ready, b * STAT_N + stat_no[s] + 1)
                    else:
                        pe.wait_ge(hT_ready, b * HT_N + hT_no[s] + 1)

                def do_step(step):
                    name, p, c = step
                    if name == "fold":
                        return
                    m = use[step]
                    slot_ready(m)
                    if name == "rows":
                        n = fold_no[("fold", p, c)]
                        if p == 3:
                            pe.wait_ge(bias_added, b * J + c + 1)
                        pe.wait_ge(fold_ready, 1 + b * FOLDS + n + 1)
                        pe.sem_inc(pe_passed, 1)
                        for k in range(TJ):
                            mm = nc.tensor.transpose(mslot(m)[:, k * C:(k + 1) * C],
                                                     fold[:, n % 2, k * P:(k + 1) * P], ident[0:C, 0:C])
                    elif name == "msg":
                        if p == 0:
                            pe.wait_ge(hT_ready, b * HT_N + hT_no[("hT", p, c)] + 1)
                        else:
                            pe.wait_ge(hT_ready, b * HT_N + hT_no[("fold", p, c)] + 1)
                        for k in range(TJ):
                            o = c * CHUNK + k * P
                            mm = nc.tensor.matmul(mslot(m)[:, k * C:(k + 1) * C], hT[:, o:o + P],
                                                  wmT[:, p, :], start=True, stop=True)
                    else:
                        pe.wait_ge(hs_ready, b * HS + J + norm_no[("rows", p, c)] + 1)
                        for k in range(2):
                            t = c * TJ + 2 * k
                            mm = nc.tensor.transpose(mslot(m)[:, k * P:(k + 1) * P],
                                                     hs[:, t:t + 2, :].rearrange("p t c -> p (t c)"), ident[:, :])
                    mm.then_inc(misc_full, 1)

                for step in first:
                    do_step(step)
                for p in range(len(PRODUCTS) + 1):
                    for g, (c, m) in enumerate(GROUPS):
                        if p < len(PRODUCTS):
                            if m == 0:
                                if p > 0 or c >= 2:
                                    last = (p, c - 2) if c >= 2 else (p - 1, c + 2)
                                    pe.wait_ge(fold_ready, 1 + b * FOLDS + fold_no[("fold",) + last] + 1)
                            pe.wait_ge(stat_ready, b * STAT_N + stat_of[(p, m)] + 1)
                            for t in range(m * TJ, (m + 1) * TJ):
                                for part, k in ((ahi, 0), (alo, 1)):
                                    end = m == J - 1 and t == T - 1 and k == 1
                                    mm = nc.tensor.matmul(pacc[c % 2][:, :], stat[:, p % 2, t, :],
                                                          part[:, t, c * CHUNK:(c + 1) * CHUNK],
                                                          start=(t == 0 and k == 0),
                                                          stop=end)
                            if m == J - 1:
                                if 1 <= p <= L:
                                    mm = nc.tensor.matmul(pacc[c % 2][0:C, :], wsT[:, p - 1, :],
                                                          hT[:, c * CHUNK:(c + 1) * CHUNK],
                                                          start=False, stop=True, skip_group_check=True)
                                mm.then_inc(prod_done, 1)
                        for step in after[p][g]:
                            do_step(step)


_INS = ["x", "adj", "L0_gnn_U", "L0_gnn_w_scale"] + [f"L2_gnn_{n}{i}" for n in ("Wm", "Ws", "b") for i in range(3)]


def kernel(**inputs):
    import numpy as _np
    import concourse.bacc as _bacc
    from concourse import mybir as _mybir
    from concourse.bass_utils import run_bass_kernel_spmd as _run

    nc = _bacc.Bacc("TRN2", target_bir_lowering=False, num_devices=1, dynamic_dma_scratch_size=1024)
    arrays, args = {}, []
    for name in _INS:
        a = _np.ascontiguousarray(inputs[name])
        if a.ndim == 0:
            a = a.reshape(1, 1)
        if a.ndim == 1:
            a = a.reshape(-1, 1)
        arrays[f"in_{name}"] = a
        args.append(nc.dram_tensor(f"in_{name}", a.shape, _mybir.dt.from_np(a.dtype), kind="ExternalInput").ap())
    out = nc.dram_tensor("out", inputs["x"].shape, _mybir.dt.float32, kind="ExternalOutput").ap()
    x, adj, U, w_scale = args[:4]
    graph_stack(nc, x, adj, U, w_scale, args[4:7], args[7:10], args[10:13], out)
    return _run(nc, [arrays], core_ids=[0]).results[0]["out"]
```

```python
import concourse.bass as bass
from concourse import mybir
from contextlib import ExitStack

F32 = mybir.dt.float32
F16 = mybir.dt.float16
ALU = mybir.AluOpType
ACT = mybir.ActivationFunctionType
AX = mybir.AxisListType

P = 128
CHUNK = 512
LN_EPS = 1e-05
DEG_EPS = 1e-12

A_SCALE = 2.0 ** 8
U_SCALE = 2.0 ** 5
LO = 2.0 ** 11
T_DEG, T_NORM, T_CONV = 8, 0, 4
VECTOR_STEPS = 299

MEAN, CONV0, CONV1, CONV2, MESSAGES = range(5)
K_PRODUCT = -1
STAT_SLOT = [0, 1, 0, 1, 2]

PLAIN = [(c, m) for c in range(4) for m in range(4)]
LATE = [(0, 0), (0, 1), (0, 2), (1, 0), (1, 1), (1, 2), (0, 3), (1, 3)] + PLAIN[8:]
FOLLOW = {
    MEAN: (("fold", "rows", "turn", "msg"), [(4, 5, 8, 9), (8, 9, 12, 13), (12, 13, 16, 17), (16, 17, 20, 21)]),
    CONV0: (("fold", "msg"), [(7, 8), (8, 9), (12, 13), (16, 17)]),
    CONV1: (("fold", "msg"), [(7, 8), (8, 9), (12, 13), (16, 17)]),
    CONV2: (("fold", "rows"), [(7, 8), (8, 9), (12, 13), (16, 17)]),
    MESSAGES: (("fold", "rows"), [(7, 8), (8, 9), (12, 13), (15, 15)]),
}


def k_steps():
    steps = []
    for q in range(64):
        steps.append([("kchunk", q)])
        i = q // 4 - 1
        if i >= 0:
            steps[-1] += {0: [("degree", i)], 1: [("scale", i)], 2: [("kprod", i)]}.get(q % 4, [])
    steps.append([("ktail",), ("degree", 15)])
    steps.append([("scale", 15), ("kprod", 15)])
    return steps


def head_schedule():
    steps = [("norm0", c) for c in range(4)]
    for part in k_steps():
        steps += part
    for c in range(4):
        steps.append(("fold", K_PRODUCT, c))
        steps.append(("rows", K_PRODUCT, c))
    return steps + [("fill", c, i) for c in (0, 1) for i in range(16)]


def body_schedule(more):
    behind = [[] for _ in range(5 * 16 + 16)]
    for p, (names, at) in FOLLOW.items():
        for c in range(4):
            for name, g in zip(names, at[c]):
                behind[16 * p + g].append((name, p, c))
    for n in range(32):
        behind[n // 4].append(("fill", 2 + n // 16, n % 16))
    if more:
        for c in range(4):
            behind[8 + c].insert(0, ("norm0", c))
        parts = k_steps()
        first, last = 10, 66
        for n, part in enumerate(parts):
            behind[first + n * (last - first) // len(parts)] += part
        for c in range(4):
            behind[67 + 2 * c].append(("fold", K_PRODUCT, c))
            behind[68 + 2 * c].append(("rows", K_PRODUCT, c))
        for n in range(32):
            behind[75 + n // 7].append(("fill", n // 16, n % 16))
    steps = [("swap",)]
    for p in range(5):
        for g, (c, m) in enumerate(PLAIN if p == MEAN else LATE):
            steps.append(("group", p, c, m))
            steps += behind[16 * p + g]
    for late in behind[80:]:
        steps += late
    return steps


def is_norm(s):
    return s[0] == "norm0" or (s[0] == "rows" and s[1] in (K_PRODUCT, MEAN, CONV2))


def is_stat(s):
    return s[0] == "msg" or (s[0] == "rows" and s[1] in (K_PRODUCT, CONV2))


def is_hT(s):
    return s[0] == "turn" or (s[0] == "fold" and s[1] in (CONV0, CONV1))


def is_post(s):
    return s[0] in ("rows", "turn", "msg")


def alpha(p):
    return 2.0 ** (T_DEG if p == K_PRODUCT else T_CONV if p in (CONV0, CONV1, CONV2) else T_NORM) / A_SCALE


class Counts:

    KINDS = {"fold": lambda s: s[0] == "fold", "rows": lambda s: s[0] == "rows", "norm": is_norm,
             "stat": is_stat, "hT": is_hT, "post": is_post}

    def __init__(self, steps, before):
        self.steps, self.before = steps, before
        self.index = {k: {s: n for n, s in enumerate(s for s in steps if f(s))} for k, f in self.KINDS.items()}
        self.uses = [u for s in steps for u in ([("logits", s[1]), ("strip", s[1])] if s[0] == "kchunk"
                                                else [s] if is_post(s) else [])]
        self.use = {u: n for n, u in enumerate(self.uses)}

    def total(self, kind):
        return len(self.index[kind])

    def upto(self, kind, step):
        return self.before[kind] + (self.index[kind][step] + 1)

    def nth(self, kind, step):
        return self.index[kind][step]


def graph_stack(nc, x, adj, U, w_scale, wm, ws, bias, out):
    B, N, C = x.shape
    R = U.shape[1]
    T = N // P
    J = N // CHUNK
    TJ = T // J
    H = N // 2
    L = len(wm)
    CH = T * J
    PER_SLOT = 24

    x_v = x.rearrange("b (t p) c -> b p t c", p=P)
    out_v = out.rearrange("b (t p) c -> b p t c", p=P)

    head, body, tail = head_schedule(), body_schedule(True), body_schedule(False)
    zero = {k: 0 for k in Counts.KINDS}
    of_head = Counts(head, zero)

    def counts_of(steps, b):
        base = Counts(body, zero)
        return Counts(steps,
                      {k: of_head.total(k) + b * base.total(k) for k in Counts.KINDS})

    nc.disable_value_cache = True
    ctx = ExitStack()
    with ctx:
        def sb(name, shape, dt=F32):
            return ctx.enter_context(nc.sbuf_tensor(name, shape, dt))

        def pb(name):
            return ctx.enter_context(nc.psum_tensor(name, [P, CHUNK], F32))

        def sem(name):
            return ctx.enter_context(nc.semaphore(name))

        ahi = sb("ahi", [P, T, N], F16)
        alo = sb("alo", [P, T, N], F16)
        stage = sb("stage", [P, 4, H])
        tsum = sb("tsum", [P, 2, CHUNK])
        kraw = sb("kraw", [P, 3, CHUNK])
        khi = sb("khi", [P, 6, CHUNK], F16)
        klo = sb("klo", [P, 6, CHUNK], F16)
        stat = sb("stat", [P, 3, T, 2 * C], F16)
        statk = sb("statk", [P, 2, 2 * C], F16)
        xn = sb("xn", [P, T, C])
        hs = sb("hs", [P, T, C])
        xk = sb("xk", [P, T, C])
        hk = sb("hk", [P, T, C])
        hT = sb("hT", [C, N])
        uleft = sb("uleft", [4 * R, N], F16)
        uright = sb("uright", [4 * R, N], F16)
        fold = sb("fold", [C, 2, CHUNK])
        tmp = sb("tmp", [P, TJ, C])
        tmp2 = sb("tmp2", [P, TJ, C])
        xs = sb("xs", [P, C])
        ident = sb("ident", [P, P])
        small = sb("small", [P, 5, TJ])
        tiny = sb("tiny", [P, 4])
        kdeg = sb("kdeg", [P, T, J])
        rsum = sb("rsum", [P, T, 2])
        coef0 = sb("coef0", [P, T])
        coef1 = sb("coef1", [P, T])
        coef3 = sb("coef3", [P, T])
        wmT = sb("wmT", [C, L, C])
        wsT = sb("wsT", [C, L, C])
        bcol = sb("bcol", [C, L])
        wtwo = sb("wtwo", [P, 1])
        wraw = tsum[0:C, 0, 0:2 * L * C].rearrange("c (k o) -> c k o", o=C)
        uraw = tsum[:, 1, 0:T * R].rearrange("p (t r) -> p t r", r=R)
        ucat = hs[:, :, :].rearrange("p t c -> p (t c)").bitcast(F16)\
            .rearrange("p (s t k r) -> p s t k r", s=2, t=T, k=4)
        ones, w1 = tmp[0:1, 0:2, :].rearrange("p a c -> p (a c)"), tmp2[0:1, 0, 0:1]
        identh = tmp2[:, 1:2, :].rearrange("p a c -> p (a c)").bitcast(F16)

        kacc = [pb(f"kacc{j}") for j in range(J)]
        pacc = [pb(f"pacc{j}") for j in range(2)]
        work = [pb(f"work{j}") for j in range(2)]

        const_loaded = sem("constants_loaded")
        const_ready = sem("constants_ready")
        pro_pe = sem("prologue_tensor")
        pro_dve = sem("prologue_vector")
        x_loaded = sem("x_loaded")
        staged = [sem(f"slot_loaded{i}") for i in range(4)]
        stored = sem("out_stored")
        logits_ready = sem("logits_ready")
        sim_ready = sem("similarity_ready")
        summed = sem("rows_summed")
        strip_turned = sem("k_strip_turned")
        tsum_ready = sem("tsum_ready")
        k_ready = sem("k_ready")
        khi_ready = sem("khi_ready")
        klo_ready = sem("klo_ready")
        deg_ready = sem("degree_ready")
        deg_root = sem("degree_root")
        statk_ready = sem("statk_ready")
        k_used = sem("k_used")
        fill_turned = sem("a_strip_turned")
        ahi_ready = sem("ahi_ready")
        alo_ready = sem("alo_ready")
        prod_done = sem("product_chunk_done")
        lo_ready = sem("fold_lo_ready")
        fold_ready = sem("fold_ready")
        bias_added = sem("bias_added")
        ln_var = sem("variance_ready")
        ln_root = sem("variance_root")
        hs_ready = sem("normed_rows_ready")
        xhi_ready = sem("xhi_ready")
        stat_ready = sem("stationary_ready")
        hT_ready = sem("hT_ready")
        post_full = sem("work_bank_filled")
        post_read = sem("rows_read")
        swapped = sem("swapped")
        x_final = sem("x_final")
        vector_step = sem("vector_step")
        pe_passed = sem("tensor_engine_passed")

        block = ctx.enter_context(nc.Block())

        @block.sync
        def _(sp):
            for i in range(L):
                sp.dma_start(wraw[:, 2 * i, :], wm[i]).then_inc(const_loaded, 16)
                sp.dma_start(wraw[:, 2 * i + 1, :], ws[i]).then_inc(const_loaded, 16)
                sp.dma_start(bcol[:, i:i + 1], bias[i]).then_inc(const_loaded, 16)
            sp.dma_start(uraw, U.rearrange("(t p) r -> p t r", p=P)).then_inc(const_loaded, 16)
            sp.dma_start(w1, w_scale).then_inc(const_loaded, 16)
            sp.sem_inc(stored, 1)

            def load_k(kb, u):
                i, h = u // 2, u % 2
                if u >= 2:
                    sp.wait_ge(strip_turned, kb * CH + 2 * (u - 1))
                sp.dma_start(stage[:, u % 2, :].rearrange("p (t m) -> p t m", m=P),
                             adj[kb, h * H:(h + 1) * H, i * P:(i + 1) * P].rearrange("(t p) m -> p t m", p=P))\
                    .then_inc(staged[u % 2], 16)
                if u >= 2:
                    sp.wait_ge(tsum_ready, kb * CH + 2 * (u - 1))
                sp.dma_start(stage[:, 2 + u % 2, :], adj[kb, i * P:(i + 1) * P, h * H:(h + 1) * H])\
                    .then_inc(staged[2 + u % 2], 16)

            def load_a(fb, n):
                c, k = n // 8, n % 8
                if n == 0:
                    sp.wait_ge(strip_turned, fb * CH + CH)
                    sp.wait_ge(tsum_ready, fb * CH + CH)
                if n >= 4:
                    sp.wait_ge(fill_turned, fb * CH + 2 * (n - 3))
                sp.dma_start(stage[:, n % 4, :].rearrange("p (t m) -> p t m", m=2 * P),
                             adj[fb, c * CHUNK:(c + 1) * CHUNK, k * 2 * P:(k + 1) * 2 * P]
                             .rearrange("(t p) m -> p t m", p=P)).then_inc(staged[n % 4], 16)

            sp.dma_start(xk[:, :, :], x_v[0]).then_inc(x_loaded, 16)
            for u in range(2 * T):
                load_k(0, u)
            for n in range(16):
                load_a(0, n)

            def batch(b, more):
                for n in range(16, 32):
                    load_a(b, n)
                if more:
                    sp.wait_ge(swapped, b + 1)
                    sp.dma_start(xk[:, :, :], x_v[b + 1]).then_inc(x_loaded, 16)
                    sp.wait_ge(fill_turned, b * CH + CH)
                    for u in range(2 * T):
                        load_k(b + 1, u)
                    for n in range(16):
                        load_a(b + 1, n)
                for c in range(J):
                    sp.wait_ge(x_final, b * J + c + 1)
                    sp.dma_start(out_v[b, :, c * TJ:(c + 1) * TJ, :], xn[:, c * TJ:(c + 1) * TJ, :])\
                        .then_inc(stored, 16)

            with sp.Fori(0, B - 1) as b:
                batch(b, True)
            batch(B - 1, False)
            sp.wait_ge(stored, 1 + B * 16 * J)

        @block.gpsimd
        def _(pool):
            nc.gpsimd.memset(ident[:, :], 0.0).then_inc(const_ready, 1)
            nc.gpsimd.memset(ones, 1.0).then_inc(const_ready, 1)
            pool.wait_ge(const_ready, 2)
            nc.gpsimd.affine_select(out=ident[:, :], in_=ident[:, :], compare_op=ALU.not_equal, fill=1.0,
                                    base=0, pattern=[[-1, P]], channel_multiplier=1).then_inc(const_ready, 1)

            def multiply(kb):
                for q in range(CH):
                    pool.wait_ge(sim_ready, kb * CH + q + 1)
                    pool.wait_ge(tsum_ready, kb * CH + q + 1)
                    nc.gpsimd.tensor_tensor(kraw[:, q % 3, :], tsum[:, q % 2, :], kraw[:, q % 3, :],
                                            ALU.mult).then_inc(k_ready, 1)

            multiply(0)
            with pool.Fori(0, B - 1) as b:
                multiply(b + 1)

        @block.scalar
        def _(act):
            act.sem_inc(hT_ready, 1)

            def run(steps, n, b, kb, fills):
                def khigh(q):
                    act.wait_ge(k_ready, kb * CH + q + 1)
                    if q >= 6:
                        act.wait_ge(k_used, kb * T + (q - 6) // J + 1)
                    i, j = q // J, q % J
                    nc.scalar.activation(khi[:, q % 6, :], kraw[:, q % 3, :], ACT.Copy, scale=A_SCALE / 2,
                                         accum_out=kdeg[:, i, j:j + 1]).then_inc(khi_ready, 1)

                def root_ln(step):
                    act.wait_ge(ln_var, n.upto("norm", step))
                    nc.scalar.activation(small[:, 2, :], small[:, 1, :], ACT.Sqrt).then_inc(ln_root, 1)

                def xhigh(src, p, c):
                    nc.scalar.activation(stat[:, STAT_SLOT[p], c * TJ:(c + 1) * TJ, 0:C], src, ACT.Copy,
                                         scale=1.0 / LO).then_inc(xhi_ready, 1)

                for step in steps:
                    name = step[0]
                    if name == "norm0":
                        root_ln(step)
                    elif name == "kchunk":
                        q, u = step[1], step[1] // 2
                        if q % 2 == 0:
                            rows = stage[:, 2 + u % 2, :]
                            act.wait_ge(staged[2 + u % 2], 16 * (PER_SLOT * kb + u // 2 + 1))
                            nc.scalar.activation(rows, rows, ACT.Copy,
                                                 accum_out=rsum[:, u // 2, u % 2:u % 2 + 1]).then_inc(summed, 1)
                        if q >= 3:
                            act.wait_ge(klo_ready, kb * CH + q - 2)
                        act.wait_ge(logits_ready, kb * CH + q + 1)
                        nc.scalar.activation(kraw[:, q % 3, :], work[n.use[("logits", q)] % 2][:, :], ACT.Sigmoid,
                                             scale=1.0 / U_SCALE ** 2).then_inc(sim_ready, 1)
                        if q >= 1:
                            khigh(q - 1)
                    elif name == "ktail":
                        khigh(CH - 1)
                    elif name == "degree":
                        act.wait_ge(deg_ready, kb * T + step[1] + 1)
                        nc.scalar.activation(tiny[:, 2:3], tiny[:, 1:2], ACT.Sqrt).then_inc(deg_root, 1)
                    elif name == "fill":
                        _, c, i = step
                        f, fb = c * T + i, fills[c]
                        if i == 0 and b is not None and c < 2:
                            act.wait_ge(prod_done, 1 + b * (5 * J) + MESSAGES * J + c + 1)
                        if i == 0 and c >= 2:
                            act.wait_ge(prod_done, 1 + b * (5 * J))
                        act.wait_ge(fill_turned, fb * CH + f + 1)
                        nc.scalar.activation(ahi[:, i, c * CHUNK:(c + 1) * CHUNK], kacc[f % J][:, :], ACT.Copy,
                                             scale=A_SCALE).then_inc(ahi_ready, 1)
                    elif name == "fold":
                        _, p, c = step
                        if p == K_PRODUCT:
                            act.wait_ge(k_used, kb * T + T)
                        else:
                            act.wait_ge(prod_done, 1 + b * (5 * J) + p * J + c + 1)
                        slot = n.nth("fold", step) % 2
                        before = [s for s in steps if s[0] == "fold" and n.nth("fold", s) == n.nth("fold", step) - 2]
                        if not before:
                            if b is not None:
                                act.wait_ge(post_full, n.before["post"] + 0)
                        elif is_hT(before[0]):
                            act.wait_ge(hT_ready, 1 + n.upto("hT", before[0]))
                        else:
                            act.wait_ge(post_full, n.upto("post", ("rows",) + before[0][1:]))
                        src = kacc[c] if p == K_PRODUCT else pacc[c % 2]
                        nc.scalar.activation(fold[:, slot, :], src[C:2 * C, :], ACT.Copy,
                                             scale=alpha(p) / LO).then_inc(lo_ready, 1)
                        if is_hT(step):
                            act.wait_ge(fold_ready, n.upto("fold", step))
                            nc.scalar.activation(hT[:, c * CHUNK:(c + 1) * CHUNK], fold[:, slot, :], ACT.Relu,
                                                 bias=bcol[:, p - CONV0:p - CONV0 + 1]).then_inc(hT_ready, 1)
                        if p == CONV2:
                            act.wait_ge(fold_ready, n.upto("fold", step))
                            nc.scalar.activation(fold[:, slot, :], fold[:, slot, :], ACT.Identity,
                                                 bias=bcol[:, L - 1:L]).then_inc(bias_added, 1)
                    elif name == "rows":
                        _, p, c = step
                        if is_norm(step):
                            root_ln(step)
                        if is_stat(step):
                            act.wait_ge(hs_ready, n.upto("norm", step))
                            h = hk if p == K_PRODUCT else hs
                            xhigh(h[:, c * TJ:(c + 1) * TJ, :], p + 1, c)
                    elif name == "turn":
                        _, p, c = step
                        act.wait_ge(post_full, n.upto("post", step))
                        to = hT[:, c * CHUNK:(c + 1) * CHUNK].rearrange("c (k e n) -> c k e n", e=2, n=P)
                        bank = work[n.use[step] % 2]
                        for e in range(2):
                            last = nc.scalar.activation(
                                to[:, :, e, :], bank[e * C:(e + 1) * C, 0:2 * P].rearrange("c (k n) -> c k n", n=P),
                                ACT.Copy, scale=1.0 / LO)
                        last.then_inc(hT_ready, 1)
                    elif name == "msg":
                        _, p, c = step
                        act.wait_ge(post_full, n.upto("post", step))
                        xhigh(work[n.use[step] % 2][:, 0:TJ * C].rearrange("p (t c) -> p t c", c=C), p + 1, c)

            run(head, of_head, None, 0, (0, 0))
            with act.Fori(0, B - 1) as b:
                run(body, counts_of(body, b), b, b + 1, (b + 1, b + 1, b, b))
            run(tail, counts_of(tail, B - 1), B - 1, None, (None, None, B - 1, B - 1))

        @block.vector
        def _(dve):
            dve.wait_ge(const_loaded, 16 * (3 * L + 2))
            dve.wait_ge(const_ready, 3)
            for s, kinds in ((0, "hlhl"), (1, "hhll")):
                for k, kind in enumerate(kinds):
                    if kind == "h":
                        nc.vector.tensor_scalar(ucat[:, s, :, k, :], uraw, U_SCALE, None, ALU.mult)\
                            .then_inc(pro_dve, 1)
            dve.wait_ge(pro_dve, 4)
            for s, kinds in ((0, "hlhl"), (1, "hhll")):
                for k, kind in enumerate(kinds):
                    if kind == "l":
                        nc.vector.scalar_tensor_tensor(ucat[:, s, :, k, :], uraw, U_SCALE, ucat[:, s, :, 0, :],
                                                       ALU.mult, ALU.subtract).then_inc(pro_dve, 1)
            dve.wait_ge(pro_pe, 1)
            nc.vector.tensor_copy(identh, ident[:, :]).then_inc(pro_dve, 1)
            for i in range(L):
                nc.vector.tensor_scalar(wmT[:, i, :], pacc[0][0:C, 2 * i * C:(2 * i + 1) * C],
                                        LO / 2.0 ** T_CONV, None, ALU.mult).then_inc(pro_dve, 1)
                nc.vector.tensor_scalar(wsT[:, i, :], pacc[0][0:C, (2 * i + 1) * C:(2 * i + 2) * C],
                                        A_SCALE / 2.0 ** T_CONV, None, ALU.mult).then_inc(pro_dve, 1)
            nc.vector.tensor_scalar(wtwo[:, :], pacc[1][:, 0:1], 2.0, None, ALU.mult).then_inc(pro_dve, 1)
            for k in range(4):
                dve.wait_ge(pro_pe, 2 + k)
                to = (uleft, uright)[k // 2]
                nc.vector.tensor_copy(to[:, (k % 2) * H:(k % 2 + 1) * H], kacc[k][0:4 * R, :].bitcast(F16))\
                    .then_inc(pro_dve, 1)
            dve.wait_ge(pro_dve, 9 + 2 * L + 5)

            def run(steps, n, b, kb, fills, ahead):
                count = [0]

                def then(ins):
                    count[0] += 1
                    ins.then_inc(vector_step, 1)
                    dve.wait_ge(vector_step, ahead + count[0])

                def half_rstd(v, s, r, t):
                    then(nc.vector.reciprocal(r, s))
                    then(nc.vector.tensor_tensor(t, v, r, ALU.mult))
                    then(nc.vector.tensor_tensor(t, t, s, ALU.add))
                    then(nc.vector.reciprocal(r, t))

                def wide(v):
                    return v.unsqueeze(2).to_broadcast([P, TJ, C])

                def norm(step, xc, hc):
                    s0, s1, s2, s3, s4 = (small[:, k, :] for k in range(5))
                    then(nc.vector.tensor_reduce(s0, xc, AX.X, ALU.add))
                    then(nc.vector.tensor_scalar(s3, s0, -1.0 / C, None, ALU.mult))
                    then(nc.vector.tensor_tensor(hc, xc, wide(s3), ALU.add))
                    then(nc.vector.tensor_tensor(tmp[:, :, :], hc, hc, ALU.mult))
                    then(nc.vector.tensor_reduce(s0, tmp[:, :, :], AX.X, ALU.add))
                    nc.vector.tensor_scalar(s1, s0, 1.0 / C, LN_EPS, ALU.mult, ALU.add).then_inc(ln_var, 1)
                    dve.wait_ge(ln_root, n.upto("norm", step))
                    half_rstd(s1, s2, s3, s4)
                    then(nc.vector.tensor_tensor(hc, hc, wide(s3), ALU.mult))
                    nc.vector.tensor_scalar(hc, hc, 0.0, 2.0 * LO, ALU.max, ALU.mult).then_inc(hs_ready, 1)
                    dve.wait_ge(hs_ready, n.upto("norm", step))

                def klow(q):
                    dve.wait_ge(khi_ready, kb * CH + q + 1)
                    nc.vector.scalar_tensor_tensor(klo[:, q % 6, :], kraw[:, q % 3, :], A_SCALE / 2, khi[:, q % 6, :],
                                                   ALU.mult, ALU.subtract).then_inc(klo_ready, 1)

                def degree(i):
                    dve.wait_ge(khi_ready, kb * CH + J * i + J)
                    then(nc.vector.tensor_reduce(tiny[:, 0:1], kdeg[:, i, :], AX.X, ALU.add))
                    nc.vector.tensor_scalar(tiny[:, 1:2], tiny[:, 0:1], 1.0 / A_SCALE, DEG_EPS,
                                            ALU.mult, ALU.max).then_inc(deg_ready, 1)

                def scale(i):
                    dve.wait_ge(deg_root, kb * T + i + 1)
                    half_rstd(tiny[:, 1:2], tiny[:, 2:3], coef0[:, i:i + 1], tiny[:, 3:4])
                    then(nc.vector.tensor_scalar(xs[:, :], hk[:, i, :], coef0[:, i:i + 1],
                                                 2.0 / 2.0 ** T_DEG, ALU.mult, ALU.mult))
                    if i >= 2:
                        dve.wait_ge(k_used, kb * T + i - 1)
                    then(nc.vector.tensor_scalar(statk[:, i % 2, 0:C], xs[:, :], 1.0 / LO, None, ALU.mult))
                    nc.vector.scalar_tensor_tensor(statk[:, i % 2, C:2 * C], statk[:, i % 2, 0:C], -LO,
                                                   xs[:, :], ALU.mult, ALU.add).then_inc(statk_ready, 1)

                def read(step, ins):
                    ins.then_inc(post_read, 1)
                    dve.wait_ge(post_read, n.upto("rows", step))

                for step in steps:
                    name = step[0]
                    if name == "swap":
                        dve.wait_ge(stored, 1 + b * (16 * J))
                        then(nc.vector.tensor_copy(xn[:, :, :], xk[:, :, :]))
                        nc.vector.tensor_copy(hs[:, :, :], hk[:, :, :]).then_inc(swapped, 1)
                        dve.wait_ge(summed, b * (2 * T) + 2 * T)
                        then(nc.vector.tensor_reduce(coef1[:, :], rsum[:, :, :], AX.X, ALU.add))
                        then(nc.vector.tensor_scalar(coef3[:, :], coef1[:, :], 1.0, None, ALU.max))
                        then(nc.vector.reciprocal(coef3[:, :], coef3[:, :]))
                        then(nc.vector.tensor_scalar(coef1[:, :], coef1[:, :], 1.0, None, ALU.add))
                        then(nc.vector.reciprocal(coef1[:, :], coef1[:, :]))
                        dve.wait_ge(swapped, b + 1)
                    elif name == "norm0":
                        c = step[1]
                        if c == 0:
                            dve.wait_ge(x_loaded, kb * 16 + 16)
                        norm(step, xk[:, c * TJ:(c + 1) * TJ, :], hk[:, c * TJ:(c + 1) * TJ, :])
                    elif name == "kchunk":
                        q, u = step[1], step[1] // 2
                        o = (q % 2) * CHUNK
                        if q >= 2:
                            dve.wait_ge(k_ready, kb * CH + q - 1)
                        dve.wait_ge(summed, kb * (2 * T) + u + 1)
                        dve.wait_ge(strip_turned, kb * CH + q + 1)
                        nc.vector.tensor_tensor(tsum[:, q % 2, :], work[n.use[("strip", q)] % 2][:, :],
                                                stage[:, 2 + u % 2, o:o + CHUNK], ALU.add).then_inc(tsum_ready, 1)
                        if q >= 2:
                            klow(q - 2)
                    elif name == "ktail":
                        klow(CH - 2)
                        klow(CH - 1)
                    elif name == "degree":
                        degree(step[1])
                    elif name == "scale":
                        scale(step[1])
                        if step[1] == T - 1:
                            dve.wait_ge(statk_ready, kb * T + T)
                            then(nc.vector.tensor_scalar(coef0[:, :], coef0[:, :], wtwo[:, 0:1], None, ALU.mult))
                    elif name == "fill":
                        _, c, i = step
                        f, fb = c * T + i, fills[c]
                        sl = slice(c * CHUNK, (c + 1) * CHUNK)
                        dve.wait_ge(ahi_ready, fb * CH + f + 1)
                        nc.vector.scalar_tensor_tensor(alo[:, i, sl], kacc[f % J][:, :], A_SCALE, ahi[:, i, sl],
                                                       ALU.mult, ALU.subtract).then_inc(alo_ready, 1)
                    elif name == "fold":
                        _, p, c = step
                        slot = n.nth("fold", step) % 2
                        dve.wait_ge(lo_ready, n.upto("fold", step))
                        src = kacc[c] if p == K_PRODUCT else pacc[c % 2]
                        nc.vector.scalar_tensor_tensor(fold[:, slot, :], src[0:C, :], alpha(p), fold[:, slot, :],
                                                       ALU.mult, ALU.add).then_inc(fold_ready, 1)
                    elif name == "rows":
                        _, p, c = step
                        sl = slice(c * TJ, (c + 1) * TJ)
                        y = work[n.use[step] % 2][:, 0:TJ * C].rearrange("p (t c) -> p t c", c=C)
                        xc, hc = (xk, hk) if p == K_PRODUCT else (xn, hs)
                        xc, hc, t, t2 = xc[:, sl, :], hc[:, sl, :], tmp[:, :, :], tmp2[:, :, :]
                        dve.wait_ge(post_full, n.upto("post", step))
                        if p == K_PRODUCT:
                            read(step, nc.vector.tensor_tensor(t, y, wide(coef0[:, sl]), ALU.mult))
                        elif p == MEAN:
                            read(step, nc.vector.scalar_tensor_tensor(t, hc, 1.0 / LO, y, ALU.mult, ALU.add))
                            then(nc.vector.tensor_tensor(t, t, wide(coef1[:, sl]), ALU.mult))
                            then(nc.vector.tensor_scalar(t2, t, 0.0, None, ALU.min))
                            then(nc.vector.scalar_tensor_tensor(t, t, 0.0, t2, ALU.max, ALU.add))
                        elif p == MESSAGES:
                            read(step, nc.vector.tensor_tensor(t, y, wide(coef3[:, sl]), ALU.mult))
                        if p == CONV2:
                            read(step, nc.vector.tensor_tensor(xc, xc, y, ALU.add))
                        elif p == MESSAGES:
                            nc.vector.tensor_tensor(xc, xc, t, ALU.add).then_inc(x_final, 1)
                            dve.wait_ge(x_final, b * J + c + 1)
                        else:
                            then(nc.vector.tensor_tensor(xc, xc, t, ALU.add))
                        if is_norm(step):
                            norm(step, xc, hc)
                    if is_stat(step):
                        _, p, c = step
                        sl = slice(c * TJ, (c + 1) * TJ)
                        dve.wait_ge(xhi_ready, n.upto("stat", step))
                        st = stat[:, STAT_SLOT[p + 1], sl, :]
                        if name == "msg":
                            src = work[n.use[step] % 2][:, 0:TJ * C].rearrange("p (t c) -> p t c", c=C)
                        else:
                            src = (hk if p == K_PRODUCT else hs)[:, sl, :]
                        nc.vector.scalar_tensor_tensor(st[:, :, C:2 * C], st[:, :, 0:C], -LO, src,
                                                       ALU.mult, ALU.add).then_inc(stat_ready, 1)
                return count[0]

            in_head = run(head, of_head, None, 0, (0, 0), 0)
            with dve.Fori(0, B - 1) as b:
                steps = run(body, counts_of(body, b), b, b + 1, (b + 1, b + 1, b, b), b * VECTOR_STEPS + in_head)
                assert steps == VECTOR_STEPS, steps
            run(tail, counts_of(tail, B - 1), B - 1, None, (None, None, B - 1, B - 1),
                (B - 1) * VECTOR_STEPS + in_head)

        @block.tensor
        def _(pe):
            pe.wait_ge(const_loaded, 16 * (3 * L + 2))
            pe.wait_ge(const_ready, 3)
            for k in range(2 * L):
                nc.tensor.transpose(pacc[0][0:C, k * C:(k + 1) * C], wraw[:, k, :], ident[0:C, 0:C])
            nc.tensor.matmul(pacc[1][:, 0:1], ones, w1, start=True, stop=True).then_inc(pro_pe, 1)
            pe.wait_ge(pro_dve, 9)
            for k in range(4):
                for t in range(T // 2):
                    mm = nc.tensor.transpose(kacc[k][0:4 * R, :].bitcast(F16)[:, t * P:(t + 1) * P],
                                             ucat[:, k // 2, (k % 2) * (T // 2) + t, :, :]
                                             .rearrange("p k r -> p (k r)"), identh)
                mm.then_inc(pro_pe, 1)
            pe.wait_ge(pro_dve, 9 + 2 * L + 5)
            pe.sem_inc(prod_done, 1)

            def run(steps, n, b, kb, fills):
                def bank_for(use):
                    k = n.use[use]
                    if k >= 2:
                        last = n.uses[k - 2]
                        if last[0] == "logits":
                            pe.wait_ge(sim_ready, kb * CH + last[1] + 1)
                        elif last[0] == "strip":
                            pe.wait_ge(tsum_ready, kb * CH + last[1] + 1)
                        elif last[0] == "rows":
                            pe.wait_ge(post_read, n.upto("rows", last))
                        elif last[0] == "msg":
                            pe.wait_ge(stat_ready, n.upto("stat", last))
                        else:
                            pe.wait_ge(hT_ready, 1 + n.upto("hT", last))
                    elif b is not None:
                        pe.wait_ge(post_read, n.before["rows"])
                    return work[k % 2]

                for step in steps:
                    name = step[0]
                    if name == "kchunk":
                        q, u = step[1], step[1] // 2
                        i, j = q // J, q % J
                        bank = bank_for(("logits", q))
                        nc.tensor.matmul(bank[:, :], uleft[:, i * P:(i + 1) * P], uright[:, j * CHUNK:(j + 1) * CHUNK],
                                         start=True, stop=True).then_inc(logits_ready, 1)
                        bank = bank_for(("strip", q))
                        if q % 2 == 0:
                            pe.wait_ge(staged[u % 2], 16 * (PER_SLOT * kb + u // 2 + 1))
                        for k in range(TJ):
                            o = ((q % 2) * TJ + k) * P
                            mm = nc.tensor.transpose(bank[:, k * P:(k + 1) * P], stage[:, u % 2, o:o + P], ident[:, :])
                        mm.then_inc(strip_turned, 1)
                    elif name == "kprod":
                        i = step[1]
                        if i == 0 and b is not None:
                            pe.wait_ge(alo_ready, b * CH + CH)
                        pe.wait_ge(statk_ready, kb * T + i + 1)
                        pe.wait_ge(klo_ready, kb * CH + (i + 1) * J)
                        for part, k in ((khi, 0), (klo, 1)):
                            for j in range(J):
                                mm = nc.tensor.matmul(kacc[j][:, :], statk[:, i % 2, :], part[:, (i * J + j) % 6, :],
                                                      start=(i == 0 and k == 0), stop=(i == T - 1 and k == 1))
                        mm.then_inc(k_used, 1)
                    elif name == "fill":
                        _, c, i = step
                        f, fb = c * T + i, fills[c]
                        if f >= J:
                            pe.wait_ge(alo_ready, fb * CH + f - J + 1)
                        elif f == 0:
                            pe.wait_ge(fold_ready, n.upto("fold", ("fold", K_PRODUCT, J - 1)))
                        s = f // 2
                        if f % 2 == 0:
                            pe.wait_ge(staged[s % 4], 16 * (PER_SLOT * fb + 16 + s // 4 + 1))
                        for k in range(TJ):
                            o = k * 2 * P + (f % 2) * P
                            mm = nc.tensor.transpose(kacc[f % J][:, k * P:(k + 1) * P], stage[:, s % 4, o:o + P],
                                                     ident[:, :])
                        mm.then_inc(fill_turned, 1)
                    elif name == "rows":
                        _, p, c = step
                        bank = bank_for(step)
                        if p == CONV2:
                            pe.wait_ge(bias_added, b * J + c + 1)
                        pe.wait_ge(fold_ready, n.upto("fold", ("fold", p, c)))
                        pe.sem_inc(pe_passed, 1)
                        slot = n.nth("fold", ("fold", p, c)) % 2
                        for k in range(TJ):
                            mm = nc.tensor.transpose(bank[:, k * C:(k + 1) * C],
                                                     fold[:, slot, k * P:(k + 1) * P], ident[0:C, 0:C])
                        mm.then_inc(post_full, 1)
                    elif name == "turn":
                        _, p, c = step
                        bank = bank_for(step)
                        pe.wait_ge(hs_ready, n.upto("norm", ("rows", p, c)))
                        for k in range(2):
                            t = c * TJ + 2 * k
                            mm = nc.tensor.transpose(bank[:, k * P:(k + 1) * P],
                                                     hs[:, t:t + 2, :].rearrange("p t c -> p (t c)"), ident[:, :])
                        mm.then_inc(post_full, 1)
                    elif name == "msg":
                        _, p, c = step
                        bank = bank_for(step)
                        made = ("turn" if p == MEAN else "fold", p, c)
                        pe.wait_ge(hT_ready, 1 + n.upto("hT", made))
                        for k in range(TJ):
                            o = c * CHUNK + k * P
                            mm = nc.tensor.matmul(bank[:, k * C:(k + 1) * C], hT[:, o:o + P], wmT[:, p, :],
                                                  start=True, stop=True)
                        mm.then_inc(post_full, 1)
                    elif name == "group":
                        _, p, c, m = step
                        bank = pacc[c % 2]
                        if m == 0 and (p, c) not in ((0, 0), (0, 1)):
                            last = (p, c - 2) if c >= 2 else (p - 1, c + 2)
                            pe.wait_ge(fold_ready, n.upto("fold", ("fold",) + last))
                        if p == MEAN:
                            if c == 0 and m == 0:
                                pe.wait_ge(fold_ready, n.before["fold"])
                                pe.wait_ge(stat_ready, n.before["stat"])
                            if m == 0:
                                pe.wait_ge(alo_ready, b * CH + (c + 1) * T)
                        else:
                            made = ("msg", p - 1, m) if p <= CONV2 else ("rows", p - 1, m)
                            pe.wait_ge(stat_ready, n.upto("stat", made))
                        for t in range(m * TJ, (m + 1) * TJ):
                            for part, k in ((ahi, 0), (alo, 1)):
                                mm = nc.tensor.matmul(bank[:, :], stat[:, STAT_SLOT[p], t, :],
                                                      part[:, t, c * CHUNK:(c + 1) * CHUNK],
                                                      start=(t == 0 and k == 0), stop=(t == T - 1 and k == 1))
                        if m == J - 1:
                            if CONV0 <= p <= CONV2:
                                mm = nc.tensor.matmul(bank[0:C, :], wsT[:, p - CONV0, :],
                                                      hT[:, c * CHUNK:(c + 1) * CHUNK],
                                                      start=False, stop=True, skip_group_check=True)
                            mm.then_inc(prod_done, 1)

            run(head, of_head, None, 0, (0, 0))
            with pe.Fori(0, B - 1) as b:
                run(body, counts_of(body, b), b, b + 1, (b + 1, b + 1, b, b))
            run(tail, counts_of(tail, B - 1), B - 1, None, (None, None, B - 1, B - 1))


_INS = ["x", "adj", "L0_gnn_U", "L0_gnn_w_scale"] + [f"L2_gnn_{n}{i}" for n in ("Wm", "Ws", "b") for i in range(3)]


def kernel(**inputs):
    import numpy as _np
    import concourse.bacc as _bacc
    from concourse import mybir as _mybir
    from concourse.bass_utils import run_bass_kernel_spmd as _run

    nc = _bacc.Bacc("TRN2", target_bir_lowering=False, num_devices=1, dynamic_dma_scratch_size=1024)
    arrays, args = {}, []
    for name in _INS:
        a = _np.ascontiguousarray(inputs[name])
        if a.ndim == 0:
            a = a.reshape(1, 1)
        if a.ndim == 1:
            a = a.reshape(-1, 1)
        arrays[f"in_{name}"] = a
        args.append(nc.dram_tensor(f"in_{name}", a.shape, _mybir.dt.from_np(a.dtype), kind="ExternalInput").ap())
    out = nc.dram_tensor("out", inputs["x"].shape, _mybir.dt.float32, kind="ExternalOutput").ap()
    x, adj, U, w_scale = args[:4]
    graph_stack(nc, x, adj, U, w_scale, args[4:7], args[7:10], args[10:13], out)
    return _run(nc, [arrays], core_ids=[0]).results[0]["out"]
```

```python
import concourse.bass as bass
from concourse import mybir
from contextlib import ExitStack

F32 = mybir.dt.float32
F16 = mybir.dt.float16
I32 = mybir.dt.int32
ALU = mybir.AluOpType
ACT = mybir.ActivationFunctionType
AX = mybir.AxisListType

P = 128
CHUNK = 512
LN_EPS = 1e-05
DEG_EPS = 1e-12
RSQRT_BITS = float(0x5F3759DF)

A_SCALE = 2.0 ** 8
U_SCALE = 2.0 ** 5
LO = 2.0 ** 11
T_DEG, T_NORM, T_CONV = 8, 0, 4
D_SCALE = 2.0 ** -T_DEG

SUMS, SIMS, SPLITS = 3, 4, 8
HIGH_LAG, LOW_LAG = 2, 3
DEGREE_LAG, SCALE_LAG, PROD_LAG = 6, 8, 10

NORM_STEPS = 28
VECTOR_STEPS = 275

MEAN, CONV0, CONV1, CONV2, MESSAGES = range(5)
K_PRODUCT = -1
STAT_SLOT = [0, 1, 0, 1, 2]

GROUPS = 32
PLAIN = [(c, m) for c in range(4) for m in range(8)]
LATE = PLAIN[0:4] + PLAIN[8:12] + PLAIN[4:6] + PLAIN[12:14] + PLAIN[6:8] + PLAIN[14:]
FOLLOW = {
    MEAN: (("fold", "rows", "variance", "norm", "turn", "msg"),
        [(9, 11, 13, 15, 19, 21), (17, 19, 21, 23, 27, 29), (25, 27, 29, 31, 35, 37), (33, 35, 36, 38, 41, 41)]),
    CONV0: (("fold", "relu", "msg"), [(15, 17, 18), (17, 19, 20), (25, 27, 28), (33, 35, 36)]),
    CONV1: (("fold", "relu", "msg"), [(15, 17, 18), (17, 19, 20), (25, 27, 28), (33, 35, 36)]),
    CONV2: (("fold", "rows", "variance", "norm", "stat"),
        [(15, 17, 18, 20, 25), (17, 20, 21, 23, 28), (25, 27, 28, 30, 35), (33, 35, 36, 38, 42)]),
    MESSAGES: (("fold", "rows"), [(15, 17), (17, 19), (25, 27), (31, 31)]),
}
K_SPAN = (27, 136)
K_FOLDS = (137, 139, 143, 147)
K_ROWS = (139, 141, 145, 147)
K_STATS = (159, 160, 166, 166)
FILL_AT, FILL_EVERY = 151, 3
FILL2_EVERY, FILL3_AT, FILL3_EVERY = 2, 8, 4


def k_steps():
    steps = []
    for q in range(64):
        steps.append([("kchunk", q)])
        for name, lag in (("scale", SCALE_LAG), ("kprod", PROD_LAG)):
            if q >= lag and (q - lag) % 4 == 0:
                steps[-1].append((name, (q - lag) // 4))
    return steps + [[("scale", 14)], [("ktail",), ("kprod", 14)], [], [("scale", 15)], [], [("kprod", 15)]]


def head_schedule():
    steps = []
    for part in k_steps():
        steps += part
    for c in range(4):
        steps.append(("fold", K_PRODUCT, c))
        steps.append(("rows", K_PRODUCT, c))
    steps += [("fill", c, i) for c in (0, 1) for i in range(16)]
    return steps + [("stat", K_PRODUCT, c) for c in range(4)]


def body_schedule(more):
    behind = [[] for _ in range(6 * GROUPS)]
    for p, (names, at) in FOLLOW.items():
        for c in range(4):
            for name, g in zip(names, at[c]):
                behind[GROUPS * p + g].append((name, p, c))
    for n in range(32):
        at = n // FILL2_EVERY if n < 16 else FILL3_AT + (n - 16) // FILL3_EVERY
        behind[at].append(("fill", 2 + n // 16, n % 16))
    if more:
        parts = k_steps()
        first, last = K_SPAN
        for n, part in enumerate(parts):
            behind[first + n * (last - first) // len(parts)] += part
        for c in range(4):
            behind[K_FOLDS[c]].append(("fold", K_PRODUCT, c))
            behind[K_ROWS[c]].append(("rows", K_PRODUCT, c))
            behind[K_STATS[c]].append(("stat", K_PRODUCT, c))
        for n in range(32):
            behind[FILL_AT + n // FILL_EVERY].append(("fill", n // 16, n % 16))
    steps = [("swap",)]
    for p in range(5):
        for g, (c, m) in enumerate(PLAIN if p == MEAN else LATE):
            steps.append(("group", p, c, m))
            steps += behind[GROUPS * p + g]
    for late in behind[5 * GROUPS:]:
        steps += late
    return steps


def is_norm(s):
    return s[0] == "norm"


def is_stat(s):
    return s[0] in ("msg", "stat")


def is_hT(s):
    return s[0] in ("turn", "relu")


def is_post(s):
    return s[0] in ("rows", "turn", "msg")


def alpha(p):
    return 2.0 ** (T_DEG if p == K_PRODUCT else T_CONV if p in (CONV0, CONV1, CONV2) else T_NORM) / A_SCALE


class Counts:

    KINDS = {"fold": lambda s: s[0] == "fold", "rows": lambda s: s[0] == "rows", "norm": is_norm,
             "stat": is_stat, "hT": is_hT, "post": is_post}

    def __init__(self, steps, before):
        self.steps, self.before = steps, before
        self.index = {k: {s: n for n, s in enumerate(s for s in steps if f(s))} for k, f in self.KINDS.items()}
        self.uses = [u for s in steps for u in ([("logits", s[1]), ("strip", s[1])] if s[0] == "kchunk"
                                                else [s] if is_post(s) else [])]
        self.use = {u: n for n, u in enumerate(self.uses)}

    def total(self, kind):
        return len(self.index[kind])

    def upto(self, kind, step):
        return self.before[kind] + (self.index[kind][step] + 1)

    def nth(self, kind, step):
        return self.index[kind][step]


def graph_stack(nc, x, adj, U, w_scale, wm, ws, bias, out):
    B, N, C = x.shape
    R = U.shape[1]
    T = N // P
    J = N // CHUNK
    TJ = T // J
    H = N // 2
    L = len(wm)
    CH = T * J
    PER_SLOT = 24

    x_v = x.rearrange("b (t p) c -> b p t c", p=P)
    out_v = out.rearrange("b (t p) c -> b p t c", p=P)

    head, body, tail = head_schedule(), body_schedule(True), body_schedule(False)
    zero = {k: 0 for k in Counts.KINDS}
    of_head = Counts(head, zero)

    def counts_of(steps, b):
        base = Counts(body, zero)
        return Counts(steps,
                      {k: of_head.total(k) + b * base.total(k) for k in Counts.KINDS})

    nc.disable_value_cache = True
    ctx = ExitStack()
    with ctx:
        def sb(name, shape, dt=F32):
            return ctx.enter_context(nc.sbuf_tensor(name, shape, dt))

        def pb(name):
            return ctx.enter_context(nc.psum_tensor(name, [P, CHUNK], F32))

        def sem(name):
            return ctx.enter_context(nc.semaphore(name))

        ahi = sb("ahi", [P, T, N], F16)
        alo = sb("alo", [P, T, N], F16)
        stage = sb("stage", [P, 4, H])
        tsum = sb("tsum", [P, SUMS, CHUNK])
        kraw = sb("kraw", [P, SIMS, CHUNK])
        khi = sb("khi", [P, SPLITS, CHUNK], F16)
        klo = sb("klo", [P, SPLITS, CHUNK], F16)
        stat = sb("stat", [P, 3, T, 2 * C], F16)
        statk = sb("statk", [P, 2, 2 * C], F16)
        xn = sb("xn", [P, T, C])
        hs = sb("hs", [P, T, C])
        xk = sb("xk", [P, T, C])
        hk = sb("hk", [P, T, C])
        columns = sb("columns", [P, N])
        fold = sb("fold", [C, 2, CHUNK])
        tmp = sb("tmp", [P, TJ, C])
        tmp2 = sb("tmp2", [P, TJ, C])
        xs = sb("xs", [P, 2, C])
        ident = sb("ident", [P, P])
        wide_small = sb("wide_small", [P, 4, T])
        small = sb("small", [P, 5, TJ])
        tiny = sb("tiny", [P, 4])
        kdeg = sb("kdeg", [P, T, J])
        rsum = sb("rsum", [P, T, 2])
        coef0 = sb("coef0", [P, T])
        coef1 = sb("coef1", [P, T])
        coef3 = sb("coef3", [P, T])
        wmT = sb("wmT", [C, L, C])
        wsT = sb("wsT", [C, L, C])
        bcol = sb("bcol", [C, L])
        wcol = sb("wcol", [P, 1])
        hT = columns[0:C, :]
        parts = columns[C:C + 4 * R, :].bitcast(F16)
        uleft, uright = parts[:, 0:N], parts[:, N:2 * N]
        wraw = tsum[0:C, 0, 0:2 * L * C].rearrange("c (k o) -> c k o", o=C)
        uraw = tsum[:, 1, 0:T * R].rearrange("p (t r) -> p t r", r=R)
        ucat = hs[:, :, :].rearrange("p t c -> p (t c)").bitcast(F16)\
            .rearrange("p (s t k r) -> p s t k r", s=2, t=T, k=4)
        ones, w1 = tmp[0:1, 0:2, :].rearrange("p a c -> p (a c)"), tmp2[0:1, 0, 0:1]
        identh = tmp2[:, 1:2, :].rearrange("p a c -> p (a c)").bitcast(F16)

        kacc = [pb(f"kacc{j}") for j in range(J)]
        pacc = [pb(f"pacc{j}") for j in range(2)]
        work = [pb(f"work{j}") for j in range(2)]

        const_loaded = sem("constants_loaded")
        const_ready = sem("constants_ready")
        pro_pe = sem("prologue_tensor")
        pro_dve = sem("prologue_vector")
        x_loaded = sem("x_loaded")
        staged = [sem(f"slot_loaded{i}") for i in range(4)]
        stored = sem("out_stored")
        logits_ready = sem("logits_ready")
        sim_ready = sem("similarity_ready")
        summed = sem("rows_summed")
        strip_turned = sem("k_strip_turned")
        tsum_ready = sem("tsum_ready")
        k_ready = sem("k_ready")
        khi_ready = sem("khi_ready")
        klo_ready = sem("klo_ready")
        deg_ready = sem("degree_ready")
        dh_ready = sem("degree_times_rows_ready")
        dhi_ready = sem("degree_times_rows_hi_ready")
        statk_ready = sem("statk_ready")
        k_used = sem("k_used")
        fill_turned = sem("a_strip_turned")
        ahi_ready = sem("ahi_ready")
        alo_ready = sem("alo_ready")
        prod_done = sem("product_chunk_done")
        lo_ready = sem("fold_lo_ready")
        fold_ready = sem("fold_ready")
        ahead_normed = sem("ahead_normed")
        xk_ready = sem("ahead_x_ready")
        pool_step = sem("gpsimd_step")
        pool_passed = sem("gpsimd_passed")
        hs_ready = sem("normed_rows_ready")
        xhi_ready = sem("xhi_ready")
        stat_ready = sem("stationary_ready")
        hT_ready = sem("hT_ready")
        post_full = sem("work_bank_filled")
        post_read = sem("rows_read")
        swapped = sem("swapped")
        x_final = sem("x_final")
        vector_step = sem("vector_step")
        pe_passed = sem("tensor_engine_passed")

        block = ctx.enter_context(nc.Block())

        @block.sync
        def _(sp):
            for i in range(L):
                sp.dma_start(wraw[:, 2 * i, :], wm[i]).then_inc(const_loaded, 16)
                sp.dma_start(wraw[:, 2 * i + 1, :], ws[i]).then_inc(const_loaded, 16)
                sp.dma_start(bcol[:, i:i + 1], bias[i]).then_inc(const_loaded, 16)
            sp.dma_start(uraw, U.rearrange("(t p) r -> p t r", p=P)).then_inc(const_loaded, 16)
            sp.dma_start(w1, w_scale).then_inc(const_loaded, 16)
            sp.sem_inc(stored, 1)

            def load_k(kb, u):
                i, h = u // 2, u % 2
                if u >= 2:
                    sp.wait_ge(strip_turned, kb * CH + 2 * (u - 1))
                sp.dma_start(stage[:, u % 2, :].rearrange("p (t m) -> p t m", m=P),
                             adj[kb, h * H:(h + 1) * H, i * P:(i + 1) * P].rearrange("(t p) m -> p t m", p=P))\
                    .then_inc(staged[u % 2], 16)
                if u >= 2:
                    sp.wait_ge(tsum_ready, kb * CH + 2 * (u - 1))
                sp.dma_start(stage[:, 2 + u % 2, :], adj[kb, i * P:(i + 1) * P, h * H:(h + 1) * H])\
                    .then_inc(staged[2 + u % 2], 16)

            def load_a(fb, n):
                c, k = n // 8, n % 8
                if n == 0:
                    sp.wait_ge(strip_turned, fb * CH + CH)
                    sp.wait_ge(tsum_ready, fb * CH + CH)
                if n >= 4:
                    sp.wait_ge(fill_turned, fb * CH + 2 * (n - 3))
                sp.dma_start(stage[:, n % 4, :].rearrange("p (t m) -> p t m", m=2 * P),
                             adj[fb, c * CHUNK:(c + 1) * CHUNK, k * 2 * P:(k + 1) * 2 * P]
                             .rearrange("(t p) m -> p t m", p=P)).then_inc(staged[n % 4], 16)

            sp.dma_start(xk[:, :, :], x_v[0]).then_inc(x_loaded, 16)
            for u in range(2 * T):
                load_k(0, u)
            for n in range(16):
                load_a(0, n)

            def batch(b, more):
                for n in range(16, 32):
                    load_a(b, n)
                    if more and n == 19:
                        sp.wait_ge(swapped, b + 1)
                        sp.dma_start(xk[:, :, :], x_v[b + 1]).then_inc(x_loaded, 16)
                if more:
                    sp.wait_ge(fill_turned, b * CH + CH)
                    for u in range(2 * T):
                        load_k(b + 1, u)
                    for n in range(16):
                        load_a(b + 1, n)
                for c in range(J):
                    sp.wait_ge(x_final, b * J + c + 1)
                    sp.dma_start(out_v[b, :, c * TJ:(c + 1) * TJ, :], xn[:, c * TJ:(c + 1) * TJ, :])\
                        .then_inc(stored, 16)

            with sp.Fori(0, B - 1) as b:
                batch(b, True)
            batch(B - 1, False)
            sp.wait_ge(stored, 1 + B * 16 * J)

        @block.gpsimd
        def _(pool):
            nc.gpsimd.memset(ident[:, :], 0.0).then_inc(const_ready, 1)
            nc.gpsimd.memset(ones, 1.0).then_inc(const_ready, 1)
            pool.wait_ge(const_ready, 2)
            nc.gpsimd.affine_select(out=ident[:, :], in_=ident[:, :], compare_op=ALU.not_equal, fill=1.0,
                                    base=0, pattern=[[-1, P]], channel_multiplier=1).then_inc(const_ready, 1)

            def norm_ahead(first, last, ahead):
                nt = last - first
                xc, hc = xk[:, first:last, :], hk[:, first:last, :]
                square = tsum[:, :, :].rearrange("p s m -> p (s m)")[:, first * C:last * C]\
                    .rearrange("p (t c) -> p t c", c=C)
                v, r, q, p = (wide_small[:, n, first:last] for n in range(4))

                def wide(a):
                    return a.unsqueeze(2).to_broadcast([P, nt, C])

                count = [0]

                def then(ins):
                    count[0] += 1
                    ins.then_inc(pool_step, 1)
                    pool.wait_ge(pool_step, ahead + count[0])
                    pool.sem_inc(pool_passed, 1)

                def sums(a):
                    w = C // 2
                    while w:
                        then(nc.gpsimd.tensor_tensor(square[:, :, 0:w], a[:, :, 0:w], a[:, :, w:2 * w], ALU.add))
                        a, w = square, w // 2

                sums(xc)
                then(nc.gpsimd.tensor_scalar(v, square[:, :, 0], -1.0 / C, None, ALU.mult))
                then(nc.gpsimd.tensor_tensor(hc, xc, wide(v), ALU.add))
                then(nc.gpsimd.tensor_tensor(square, hc, hc, ALU.mult))
                sums(square)
                then(nc.gpsimd.tensor_scalar(v, square[:, :, 0], 1.0 / C, LN_EPS, ALU.mult, ALU.add))
                then(nc.gpsimd.tensor_scalar(r.bitcast(I32), v.bitcast(I32), -0.5, RSQRT_BITS, ALU.mult, ALU.add))
                then(nc.gpsimd.tensor_tensor(q, r, r, ALU.mult))
                then(nc.gpsimd.tensor_tensor(q, q, v, ALU.mult))
                then(nc.gpsimd.tensor_scalar(p, q, 3 / 8, -5 / 4, ALU.mult, ALU.add))
                then(nc.gpsimd.tensor_tensor(p, p, q, ALU.mult))
                then(nc.gpsimd.tensor_scalar(p, p, 15 / 8, None, ALU.add))
                then(nc.gpsimd.tensor_tensor(r, p, r, ALU.mult))
                then(nc.gpsimd.tensor_tensor(q, r, r, ALU.mult))
                then(nc.gpsimd.tensor_tensor(q, q, v, ALU.mult))
                then(nc.gpsimd.tensor_scalar(q, q, -LO / 2, 3 * LO / 2, ALU.mult, ALU.add))
                then(nc.gpsimd.tensor_tensor(r, q, r, ALU.mult))
                then(nc.gpsimd.tensor_scalar(hc, hc, 0.0, None, ALU.max))
                nc.gpsimd.tensor_tensor(hc, hc, wide(r), ALU.mult).then_inc(ahead_normed, 1)
                assert count[0] == NORM_STEPS

            def ahead(kb):
                steps = kb * (3 * NORM_STEPS)
                pool.wait_ge(x_loaded, kb * 16 + 16)
                pool.sem_inc(pool_passed, 1)
                norm_ahead(0, T, steps)
                for q in range(CH):
                    pool.wait_ge(sim_ready, kb * CH + q + 1)
                    pool.wait_ge(tsum_ready, kb * CH + q + 1)
                    nc.gpsimd.tensor_tensor(kraw[:, q % SIMS, :], tsum[:, q % SUMS, :], kraw[:, q % SIMS, :],
                                            ALU.mult).then_inc(k_ready, 1)
                for k in range(2):
                    pool.wait_ge(xk_ready, kb * J + 2 * k + 2)
                    pool.sem_inc(pool_passed, 1)
                    norm_ahead(k * T // 2, (k + 1) * T // 2, steps + (1 + k) * NORM_STEPS)

            pool.wait_ge(pro_dve, 9 + 2 * L + 5)
            ahead(0)
            with pool.Fori(0, B - 1) as b:
                ahead(b + 1)

        @block.scalar
        def _(act):
            act.sem_inc(hT_ready, 1)

            def run(steps, n, b, kb, fills):
                def khigh(q):
                    act.wait_ge(k_ready, kb * CH + q + 1)
                    if q >= SPLITS:
                        act.wait_ge(k_used, kb * T + (q - SPLITS) // J + 1)
                    i, j = q // J, q % J
                    nc.scalar.activation(khi[:, q % SPLITS, :], kraw[:, q % SIMS, :], ACT.Copy, scale=A_SCALE / 2,
                                         accum_out=kdeg[:, i, j:j + 1]).then_inc(khi_ready, 1)

                def xhigh(src, p, c):
                    nc.scalar.activation(stat[:, STAT_SLOT[p], c * TJ:(c + 1) * TJ, 0:C], src, ACT.Copy,
                                         scale=1.0 / LO).then_inc(xhi_ready, 1)

                for step in steps:
                    name = step[0]
                    if name == "kchunk":
                        q, u = step[1], step[1] // 2
                        if q % 2 == 0:
                            rows = stage[:, 2 + u % 2, :]
                            act.wait_ge(staged[2 + u % 2], 16 * (PER_SLOT * kb + u // 2 + 1))
                            nc.scalar.activation(rows, rows, ACT.Copy,
                                                 accum_out=rsum[:, u // 2, u % 2:u % 2 + 1]).then_inc(summed, 1)
                        if q >= SIMS:
                            act.wait_ge(klo_ready, kb * CH + q - SIMS + 1)
                        act.wait_ge(logits_ready, kb * CH + q + 1)
                        nc.scalar.activation(kraw[:, q % SIMS, :], work[n.use[("logits", q)] % 2][:, :], ACT.Sigmoid,
                                             scale=1.0 / U_SCALE ** 2).then_inc(sim_ready, 1)
                        if q >= HIGH_LAG:
                            khigh(q - HIGH_LAG)
                    elif name == "ktail":
                        for q in range(CH - HIGH_LAG, CH):
                            khigh(q)
                    elif name == "scale":
                        i = step[1]
                        act.wait_ge(deg_ready, kb * T + i + 1)
                        if i == 0:
                            act.wait_ge(ahead_normed, kb * 3 + 1)
                        if i >= 2:
                            act.wait_ge(k_used, kb * T + i - 1)
                        nc.scalar.activation(xs[:, i % 2, :], hk[:, i, :], ACT.Copy,
                                             scale=coef0[:, i:i + 1]).then_inc(dh_ready, 1)
                        act.wait_ge(dh_ready, kb * T + i + 1)
                        nc.scalar.activation(statk[:, i % 2, 0:C], xs[:, i % 2, :], ACT.Copy,
                                             scale=1.0 / LO).then_inc(dhi_ready, 1)
                    elif name == "fill":
                        _, c, i = step
                        f, fb = c * T + i, fills[c]
                        if i == 0 and b is not None and c < 2:
                            act.wait_ge(prod_done, 1 + b * (5 * J) + MESSAGES * J + c + 1)
                        if i == 0 and c >= 2:
                            act.wait_ge(prod_done, 1 + b * (5 * J))
                        act.wait_ge(fill_turned, fb * CH + f + 1)
                        nc.scalar.activation(ahi[:, i, c * CHUNK:(c + 1) * CHUNK], kacc[f % J][:, :], ACT.Copy,
                                             scale=A_SCALE).then_inc(ahi_ready, 1)
                    elif name == "fold":
                        _, p, c = step
                        if p == K_PRODUCT:
                            act.wait_ge(k_used, kb * T + T)
                        else:
                            act.wait_ge(prod_done, 1 + b * (5 * J) + p * J + c + 1)
                        slot = n.nth("fold", step) % 2
                        before = [s for s in steps if s[0] == "fold" and n.nth("fold", s) == n.nth("fold", step) - 2]
                        if not before:
                            if b is not None:
                                act.wait_ge(post_full, n.before["post"] + 0)
                        elif before[0][1] in (CONV0, CONV1):
                            act.wait_ge(hT_ready, 1 + n.upto("hT", ("relu",) + before[0][1:]))
                        else:
                            act.wait_ge(post_full, n.upto("post", ("rows",) + before[0][1:]))
                        src = kacc[c] if p == K_PRODUCT else pacc[c % 2]
                        if p == CONV2:
                            nc.scalar.activation(fold[:, slot, :], src[C:2 * C, :], ACT.Identity,
                                                 scale=alpha(p) / LO, bias=bcol[:, L - 1:L]).then_inc(lo_ready, 1)
                        else:
                            nc.scalar.activation(fold[:, slot, :], src[C:2 * C, :], ACT.Copy,
                                                 scale=alpha(p) / LO).then_inc(lo_ready, 1)
                    elif name == "relu":
                        _, p, c = step
                        act.wait_ge(fold_ready, n.upto("fold", ("fold", p, c)))
                        nc.scalar.activation(hT[:, c * CHUNK:(c + 1) * CHUNK],
                                             fold[:, n.nth("fold", ("fold", p, c)) % 2, :], ACT.Relu,
                                             bias=bcol[:, p - CONV0:p - CONV0 + 1]).then_inc(hT_ready, 1)
                    elif name == "stat":
                        _, p, c = step
                        if p == K_PRODUCT:
                            act.wait_ge(ahead_normed, kb * 3 + 2 + c // 2)
                        else:
                            act.wait_ge(hs_ready, n.upto("norm", ("norm", p, c)))
                        xhigh((hk if p == K_PRODUCT else hs)[:, c * TJ:(c + 1) * TJ, :], p + 1, c)
                    elif name == "turn":
                        _, p, c = step
                        act.wait_ge(post_full, n.upto("post", step))
                        to = hT[:, c * CHUNK:(c + 1) * CHUNK].rearrange("c (k e n) -> c k e n", e=2, n=P)
                        bank = work[n.use[step] % 2]
                        for e in range(2):
                            last = nc.scalar.activation(
                                to[:, :, e, :], bank[e * C:(e + 1) * C, 0:2 * P].rearrange("c (k n) -> c k n", n=P),
                                ACT.Copy, scale=1.0 / LO)
                        last.then_inc(hT_ready, 1)
                    elif name == "msg":
                        _, p, c = step
                        act.wait_ge(post_full, n.upto("post", step))
                        xhigh(work[n.use[step] % 2][:, 0:TJ * C].rearrange("p (t c) -> p t c", c=C), p + 1, c)

            run(head, of_head, None, 0, (0, 0))
            with act.Fori(0, B - 1) as b:
                run(body, counts_of(body, b), b, b + 1, (b + 1, b + 1, b, b))
            run(tail, counts_of(tail, B - 1), B - 1, None, (None, None, B - 1, B - 1))

        @block.vector
        def _(dve):
            dve.wait_ge(const_loaded, 16 * (3 * L + 2))
            dve.wait_ge(const_ready, 3)
            for s, kinds in ((0, "hlhl"), (1, "hhll")):
                for k, kind in enumerate(kinds):
                    if kind == "h":
                        nc.vector.tensor_scalar(ucat[:, s, :, k, :], uraw, U_SCALE, None, ALU.mult)\
                            .then_inc(pro_dve, 1)
            dve.wait_ge(pro_dve, 4)
            for s, kinds in ((0, "hlhl"), (1, "hhll")):
                for k, kind in enumerate(kinds):
                    if kind == "l":
                        nc.vector.scalar_tensor_tensor(ucat[:, s, :, k, :], uraw, U_SCALE, ucat[:, s, :, 0, :],
                                                       ALU.mult, ALU.subtract).then_inc(pro_dve, 1)
            dve.wait_ge(pro_pe, 1)
            nc.vector.tensor_copy(identh, ident[:, :]).then_inc(pro_dve, 1)
            for i in range(L):
                nc.vector.tensor_scalar(wmT[:, i, :], pacc[0][0:C, 2 * i * C:(2 * i + 1) * C],
                                        LO / 2.0 ** T_CONV, None, ALU.mult).then_inc(pro_dve, 1)
                nc.vector.tensor_scalar(wsT[:, i, :], pacc[0][0:C, (2 * i + 1) * C:(2 * i + 2) * C],
                                        A_SCALE / 2.0 ** T_CONV, None, ALU.mult).then_inc(pro_dve, 1)
            nc.vector.tensor_copy(wcol[:, :], pacc[1][:, 0:1]).then_inc(pro_dve, 1)
            for k in range(4):
                dve.wait_ge(pro_pe, 2 + k)
                to = (uleft, uright)[k // 2]
                nc.vector.tensor_copy(to[:, (k % 2) * H:(k % 2 + 1) * H], kacc[k][0:4 * R, :].bitcast(F16))\
                    .then_inc(pro_dve, 1)
            dve.wait_ge(pro_dve, 9 + 2 * L + 5)

            def run(steps, n, b, kb, fills, ahead):
                count, started = [0], {}

                def then(ins):
                    count[0] += 1
                    ins.then_inc(vector_step, 1)
                    dve.wait_ge(vector_step, ahead + count[0])

                def later(what, ins):
                    count[0] += 1
                    ins.then_inc(vector_step, 1)
                    started[what] = count[0]

                def arrive(what):
                    dve.wait_ge(vector_step, ahead + started[what])

                def rsqrt(v, r, q, p, scale):
                    then(nc.vector.tensor_scalar(r.bitcast(I32), v.bitcast(I32), -0.5, RSQRT_BITS,
                                                 ALU.mult, ALU.add))
                    then(nc.vector.tensor_tensor(q, r, r, ALU.mult))
                    then(nc.vector.tensor_tensor(q, q, v, ALU.mult))
                    then(nc.vector.tensor_scalar(p, q, 3 / 8, -5 / 4, ALU.mult, ALU.add))
                    then(nc.vector.tensor_tensor(p, p, q, ALU.mult))
                    then(nc.vector.scalar_tensor_tensor(r, p, 15 / 8, r, ALU.add, ALU.mult))
                    then(nc.vector.tensor_tensor(q, r, r, ALU.mult))
                    then(nc.vector.scalar_tensor_tensor(q, q, -scale / 2, v, ALU.mult, ALU.mult))
                    then(nc.vector.scalar_tensor_tensor(r, q, 3 * scale / 2, r, ALU.add, ALU.mult))

                def wide(v):
                    return v.unsqueeze(2).to_broadcast([P, TJ, C])

                def variance(xc, hc):
                    s0, s1 = small[:, 0, :], small[:, 1, :]
                    then(nc.vector.tensor_reduce(s0, xc, AX.X, ALU.add))
                    then(nc.vector.scalar_tensor_tensor(hc, wide(s0), -1.0 / C, xc, ALU.mult, ALU.add))
                    then(nc.vector.tensor_tensor(tmp[:, :, :], hc, hc, ALU.mult))
                    then(nc.vector.tensor_reduce(s0, tmp[:, :, :], AX.X, ALU.add))
                    later("variance", nc.vector.tensor_scalar(s1, s0, 1.0 / C, LN_EPS, ALU.mult, ALU.add))

                def norm(step, hc):
                    s1, s2, s3, s4 = (small[:, k, :] for k in range(1, 5))
                    arrive("variance")
                    rsqrt(s1, s3, s2, s4, LO)
                    nc.vector.scalar_tensor_tensor(hc, hc, 0.0, wide(s3), ALU.max, ALU.mult)\
                        .then_inc(hs_ready, 1)
                    dve.wait_ge(hs_ready, n.upto("norm", step))

                def klow(q):
                    dve.wait_ge(khi_ready, kb * CH + q + 1)
                    nc.vector.scalar_tensor_tensor(klo[:, q % SPLITS, :], kraw[:, q % SIMS, :], A_SCALE / 2,
                                                   khi[:, q % SPLITS, :], ALU.mult, ALU.subtract).then_inc(klo_ready, 1)

                def degree(i, part):
                    v, r, q, p = tiny[:, 0:1], tiny[:, 1:2], tiny[:, 2:3], tiny[:, 3:4]
                    if part == 0:
                        dve.wait_ge(khi_ready, kb * CH + J * i + J)
                        then(nc.vector.tensor_reduce(v, kdeg[:, i, :], AX.X, ALU.add))
                        later("degree", nc.vector.tensor_scalar(v, v, 1.0 / A_SCALE, DEG_EPS, ALU.mult, ALU.max))
                        return
                    arrive("degree")
                    if part == 1:
                        then(nc.vector.tensor_scalar(r.bitcast(I32), v.bitcast(I32), -0.5, RSQRT_BITS,
                                                     ALU.mult, ALU.add))
                        later("degree", nc.vector.tensor_scalar(q, r, r, v, ALU.mult, ALU.mult))
                    elif part == 2:
                        then(nc.vector.tensor_scalar(p, q, 3 / 8, -5 / 4, ALU.mult, ALU.add))
                        then(nc.vector.tensor_scalar(p, p, q, 15 / 8, ALU.mult, ALU.add))
                        later("degree", nc.vector.tensor_tensor(r, p, r, ALU.mult))
                    else:
                        then(nc.vector.tensor_scalar(q, r, r, v, ALU.mult, ALU.mult))
                        then(nc.vector.tensor_scalar(p, q, -D_SCALE / 2, 3 * D_SCALE / 2, ALU.mult, ALU.add))
                        nc.vector.tensor_tensor(coef0[:, i:i + 1], p, r, ALU.mult).then_inc(deg_ready, 1)

                def scale(i):
                    dve.wait_ge(dhi_ready, kb * T + i + 1)
                    nc.vector.scalar_tensor_tensor(statk[:, i % 2, C:2 * C], statk[:, i % 2, 0:C], -LO,
                                                   xs[:, i % 2, :], ALU.mult, ALU.add).then_inc(statk_ready, 1)

                def read(step, ins):
                    ins.then_inc(post_read, 1)
                    dve.wait_ge(post_read, n.upto("rows", step))

                for step in steps:
                    name = step[0]
                    if name == "swap":
                        dve.wait_ge(stored, 1 + b * (16 * J))
                        then(nc.vector.tensor_copy(xn[:, :, :], xk[:, :, :]))
                        nc.vector.tensor_copy(hs[:, :, :], hk[:, :, :]).then_inc(swapped, 1)
                        dve.wait_ge(summed, b * (2 * T) + 2 * T)
                        then(nc.vector.tensor_reduce(coef1[:, :], rsum[:, :, :], AX.X, ALU.add))
                        then(nc.vector.tensor_scalar(coef3[:, :], coef1[:, :], 1.0, None, ALU.max))
                        then(nc.vector.reciprocal(coef3[:, :], coef3[:, :]))
                        then(nc.vector.tensor_scalar(coef1[:, :], coef1[:, :], 1.0, None, ALU.add))
                        then(nc.vector.reciprocal(coef1[:, :], coef1[:, :]))
                        dve.wait_ge(swapped, b + 1)
                    elif name == "kchunk":
                        q, u = step[1], step[1] // 2
                        o = (q % 2) * CHUNK
                        if q == 0:
                            dve.wait_ge(ahead_normed, kb * 3 + 1)
                        if q >= SUMS:
                            dve.wait_ge(k_ready, kb * CH + q - SUMS + 1)
                        dve.wait_ge(summed, kb * (2 * T) + u + 1)
                        dve.wait_ge(strip_turned, kb * CH + q + 1)
                        nc.vector.tensor_tensor(tsum[:, q % SUMS, :], work[n.use[("strip", q)] % 2][:, :],
                                                stage[:, 2 + u % 2, o:o + CHUNK], ALU.add).then_inc(tsum_ready, 1)
                        behind = (q - DEGREE_LAG) % J
                        i = (q - DEGREE_LAG) // J
                        if i >= 0 and behind < 2:
                            degree(i, 2 * behind)
                        if q >= LOW_LAG:
                            klow(q - LOW_LAG)
                        if i >= 0 and behind < 2:
                            degree(i, 2 * behind + 1)
                    elif name == "ktail":
                        for q in range(CH - LOW_LAG, CH - 1):
                            klow(q)
                        degree(T - 1, 0)
                        klow(CH - 1)
                        for part in range(1, 4):
                            degree(T - 1, part)
                    elif name == "scale":
                        scale(step[1])
                        if step[1] == T - 1:
                            dve.wait_ge(statk_ready, kb * T + T)
                            then(nc.vector.tensor_scalar(coef0[:, :], coef0[:, :], wcol[:, 0:1], 1.0 / D_SCALE,
                                                         ALU.mult, ALU.mult))
                    elif name == "fill":
                        _, c, i = step
                        f, fb = c * T + i, fills[c]
                        sl = slice(c * CHUNK, (c + 1) * CHUNK)
                        dve.wait_ge(ahi_ready, fb * CH + f + 1)
                        nc.vector.scalar_tensor_tensor(alo[:, i, sl], kacc[f % J][:, :], A_SCALE, ahi[:, i, sl],
                                                       ALU.mult, ALU.subtract).then_inc(alo_ready, 1)
                    elif name == "fold":
                        _, p, c = step
                        slot = n.nth("fold", step) % 2
                        dve.wait_ge(lo_ready, n.upto("fold", step))
                        src = kacc[c] if p == K_PRODUCT else pacc[c % 2]
                        nc.vector.scalar_tensor_tensor(fold[:, slot, :], src[0:C, :], alpha(p), fold[:, slot, :],
                                                       ALU.mult, ALU.add).then_inc(fold_ready, 1)
                    elif name == "rows":
                        _, p, c = step
                        sl = slice(c * TJ, (c + 1) * TJ)
                        y = work[n.use[step] % 2][:, 0:TJ * C].rearrange("p (t c) -> p t c", c=C)
                        xc, hc = (xk, hk) if p == K_PRODUCT else (xn, hs)
                        xc, hc, t = xc[:, sl, :], hc[:, sl, :], tmp[:, :, :]
                        dve.wait_ge(post_full, n.upto("post", step))
                        if p == K_PRODUCT:
                            read(step, nc.vector.tensor_tensor(t, y, wide(coef0[:, sl]), ALU.mult))
                        elif p == MEAN:
                            read(step, nc.vector.scalar_tensor_tensor(t, hc, 1.0 / LO, y, ALU.mult, ALU.add))
                            then(nc.vector.tensor_tensor(t, t, wide(coef1[:, sl]), ALU.mult))
                            then(nc.vector.scalar_tensor_tensor(xc, t, 0.0, xc, ALU.min, ALU.add))
                            then(nc.vector.scalar_tensor_tensor(xc, t, 0.0, xc, ALU.max, ALU.add))
                        elif p == MESSAGES:
                            read(step, nc.vector.tensor_tensor(t, y, wide(coef3[:, sl]), ALU.mult))
                        if p == CONV2:
                            read(step, nc.vector.tensor_tensor(xc, xc, y, ALU.add))
                        elif p == MESSAGES:
                            nc.vector.tensor_tensor(xc, xc, t, ALU.add).then_inc(x_final, 1)
                            dve.wait_ge(x_final, b * J + c + 1)
                        elif p == K_PRODUCT:
                            nc.vector.tensor_tensor(xc, xc, t, ALU.add).then_inc(xk_ready, 1)
                            dve.wait_ge(xk_ready, kb * J + c + 1)
                    elif name == "variance":
                        sl = slice(step[2] * TJ, (step[2] + 1) * TJ)
                        variance(xn[:, sl, :], hs[:, sl, :])
                    elif name == "norm":
                        norm(step, hs[:, step[2] * TJ:(step[2] + 1) * TJ, :])
                    if is_stat(step):
                        _, p, c = step
                        sl = slice(c * TJ, (c + 1) * TJ)
                        dve.wait_ge(xhi_ready, n.upto("stat", step))
                        st = stat[:, STAT_SLOT[p + 1], sl, :]
                        if name == "msg":
                            src = work[n.use[step] % 2][:, 0:TJ * C].rearrange("p (t c) -> p t c", c=C)
                        else:
                            src = (hk if p == K_PRODUCT else hs)[:, sl, :]
                        nc.vector.scalar_tensor_tensor(st[:, :, C:2 * C], st[:, :, 0:C], -LO, src,
                                                       ALU.mult, ALU.add).then_inc(stat_ready, 1)
                return count[0]

            in_head = run(head, of_head, None, 0, (0, 0), 0)
            with dve.Fori(0, B - 1) as b:
                steps = run(body, counts_of(body, b), b, b + 1, (b + 1, b + 1, b, b), b * VECTOR_STEPS + in_head)
                assert steps == VECTOR_STEPS, steps
            run(tail, counts_of(tail, B - 1), B - 1, None, (None, None, B - 1, B - 1),
                (B - 1) * VECTOR_STEPS + in_head)

        @block.tensor
        def _(pe):
            pe.wait_ge(const_loaded, 16 * (3 * L + 2))
            pe.wait_ge(const_ready, 3)
            for k in range(2 * L):
                nc.tensor.transpose(pacc[0][0:C, k * C:(k + 1) * C], wraw[:, k, :], ident[0:C, 0:C])
            nc.tensor.matmul(pacc[1][:, 0:1], ones, w1, start=True, stop=True).then_inc(pro_pe, 1)
            pe.wait_ge(pro_dve, 9)
            for k in range(4):
                for t in range(T // 2):
                    mm = nc.tensor.transpose(kacc[k][0:4 * R, :].bitcast(F16)[:, t * P:(t + 1) * P],
                                             ucat[:, k // 2, (k % 2) * (T // 2) + t, :, :]
                                             .rearrange("p k r -> p (k r)"), identh)
                mm.then_inc(pro_pe, 1)
            pe.wait_ge(pro_dve, 9 + 2 * L + 5)
            pe.sem_inc(prod_done, 1)

            def run(steps, n, b, kb, fills):
                def bank_for(use):
                    k = n.use[use]
                    if k >= 2:
                        last = n.uses[k - 2]
                        if last[0] == "logits":
                            pe.wait_ge(sim_ready, kb * CH + last[1] + 1)
                        elif last[0] == "strip":
                            pe.wait_ge(tsum_ready, kb * CH + last[1] + 1)
                        elif last[0] == "rows":
                            pe.wait_ge(post_read, n.upto("rows", last))
                        elif last[0] == "msg":
                            pe.wait_ge(stat_ready, n.upto("stat", last))
                        else:
                            pe.wait_ge(hT_ready, 1 + n.upto("hT", last))
                    elif b is not None:
                        pe.wait_ge(post_read, n.before["rows"])
                    return work[k % 2]

                for step in steps:
                    name = step[0]
                    if name == "kchunk":
                        q, u = step[1], step[1] // 2
                        i, j = q // J, q % J
                        bank = bank_for(("logits", q))
                        nc.tensor.matmul(bank[:, :], uleft[:, i * P:(i + 1) * P], uright[:, j * CHUNK:(j + 1) * CHUNK],
                                         start=True, stop=True).then_inc(logits_ready, 1)
                        bank = bank_for(("strip", q))
                        if q % 2 == 0:
                            pe.wait_ge(staged[u % 2], 16 * (PER_SLOT * kb + u // 2 + 1))
                        for k in range(TJ):
                            o = ((q % 2) * TJ + k) * P
                            mm = nc.tensor.transpose(bank[:, k * P:(k + 1) * P], stage[:, u % 2, o:o + P], ident[:, :])
                        mm.then_inc(strip_turned, 1)
                    elif name == "kprod":
                        i = step[1]
                        if i == 0 and b is not None:
                            pe.wait_ge(alo_ready, b * CH + CH)
                        pe.wait_ge(statk_ready, kb * T + i + 1)
                        pe.wait_ge(klo_ready, kb * CH + (i + 1) * J)
                        for part, k in ((khi, 0), (klo, 1)):
                            for j in range(J):
                                mm = nc.tensor.matmul(kacc[j][:, :], statk[:, i % 2, :],
                                                      part[:, (i * J + j) % SPLITS, :],
                                                      start=(i == 0 and k == 0), stop=(i == T - 1 and k == 1))
                        mm.then_inc(k_used, 1)
                    elif name == "fill":
                        _, c, i = step
                        f, fb = c * T + i, fills[c]
                        if f >= J:
                            pe.wait_ge(alo_ready, fb * CH + f - J + 1)
                        elif f == 0:
                            pe.wait_ge(fold_ready, n.upto("fold", ("fold", K_PRODUCT, J - 1)))
                        s = f // 2
                        if f % 2 == 0:
                            pe.wait_ge(staged[s % 4], 16 * (PER_SLOT * fb + 16 + s // 4 + 1))
                        for k in range(TJ):
                            o = k * 2 * P + (f % 2) * P
                            mm = nc.tensor.transpose(kacc[f % J][:, k * P:(k + 1) * P], stage[:, s % 4, o:o + P],
                                                     ident[:, :])
                        mm.then_inc(fill_turned, 1)
                    elif name == "rows":
                        _, p, c = step
                        bank = bank_for(step)
                        pe.wait_ge(fold_ready, n.upto("fold", ("fold", p, c)))
                        pe.sem_inc(pe_passed, 1)
                        slot = n.nth("fold", ("fold", p, c)) % 2
                        for k in range(TJ):
                            mm = nc.tensor.transpose(bank[:, k * C:(k + 1) * C],
                                                     fold[:, slot, k * P:(k + 1) * P], ident[0:C, 0:C])
                        mm.then_inc(post_full, 1)
                    elif name == "turn":
                        _, p, c = step
                        bank = bank_for(step)
                        pe.wait_ge(hs_ready, n.upto("norm", ("norm", p, c)))
                        for k in range(2):
                            t = c * TJ + 2 * k
                            mm = nc.tensor.transpose(bank[:, k * P:(k + 1) * P],
                                                     hs[:, t:t + 2, :].rearrange("p t c -> p (t c)"), ident[:, :])
                        mm.then_inc(post_full, 1)
                    elif name == "msg":
                        _, p, c = step
                        bank = bank_for(step)
                        made = ("turn" if p == MEAN else "relu", p, c)
                        pe.wait_ge(hT_ready, 1 + n.upto("hT", made))
                        for k in range(TJ):
                            o = c * CHUNK + k * P
                            mm = nc.tensor.matmul(bank[:, k * C:(k + 1) * C], hT[:, o:o + P], wmT[:, p, :],
                                                  start=True, stop=True)
                        mm.then_inc(post_full, 1)
                    elif name == "group":
                        _, p, c, m = step
                        bank = pacc[c % 2]
                        if m == 0 and (p, c) not in ((0, 0), (0, 1)):
                            last = (p, c - 2) if c >= 2 else (p - 1, c + 2)
                            pe.wait_ge(fold_ready, n.upto("fold", ("fold",) + last))
                        if p == MEAN:
                            if c == 0 and m == 0:
                                pe.wait_ge(fold_ready, n.before["fold"])
                                pe.wait_ge(stat_ready, n.before["stat"])
                            if m == 0:
                                pe.wait_ge(alo_ready, b * CH + (c + 1) * T)
                        else:
                            made = ("msg" if p <= CONV2 else "stat", p - 1, 2 * m // TJ)
                            pe.wait_ge(stat_ready, n.upto("stat", made))
                        for t in (2 * m, 2 * m + 1):
                            for part, k in ((ahi, 0), (alo, 1)):
                                mm = nc.tensor.matmul(bank[:, :], stat[:, STAT_SLOT[p], t, :],
                                                      part[:, t, c * CHUNK:(c + 1) * CHUNK],
                                                      start=(t == 0 and k == 0), stop=(t == T - 1 and k == 1))
                        if 2 * m + 2 == T:
                            if CONV0 <= p <= CONV2:
                                mm = nc.tensor.matmul(bank[0:C, :], wsT[:, p - CONV0, :],
                                                      hT[:, c * CHUNK:(c + 1) * CHUNK],
                                                      start=False, stop=True, skip_group_check=True)
                            mm.then_inc(prod_done, 1)

            run(head, of_head, None, 0, (0, 0))
            with pe.Fori(0, B - 1) as b:
                run(body, counts_of(body, b), b, b + 1, (b + 1, b + 1, b, b))
            run(tail, counts_of(tail, B - 1), B - 1, None, (None, None, B - 1, B - 1))


_INS = ["x", "adj", "L0_gnn_U", "L0_gnn_w_scale"] + [f"L2_gnn_{n}{i}" for n in ("Wm", "Ws", "b") for i in range(3)]


def kernel(**inputs):
    import numpy as _np
    import concourse.bacc as _bacc
    from concourse import mybir as _mybir
    from concourse.bass_utils import run_bass_kernel_spmd as _run

    nc = _bacc.Bacc("TRN2", target_bir_lowering=False, num_devices=1, dynamic_dma_scratch_size=1024)
    arrays, args = {}, []
    for name in _INS:
        a = _np.ascontiguousarray(inputs[name])
        if a.ndim == 0:
            a = a.reshape(1, 1)
        if a.ndim == 1:
            a = a.reshape(-1, 1)
        arrays[f"in_{name}"] = a
        args.append(nc.dram_tensor(f"in_{name}", a.shape, _mybir.dt.from_np(a.dtype), kind="ExternalInput").ap())
    out = nc.dram_tensor("out", inputs["x"].shape, _mybir.dt.float32, kind="ExternalOutput").ap()
    x, adj, U, w_scale = args[:4]
    graph_stack(nc, x, adj, U, w_scale, args[4:7], args[7:10], args[10:13], out)
    return _run(nc, [arrays], core_ids=[0]).results[0]["out"]
```
